# Optimizing a Trainium2 kernel written in Bass

```python
import numpy as np
import jax
import jax.numpy as jnp

def _softmax(x, axis=-1):
    return jax.nn.softmax(x, axis=axis)

def _gelu(x):
    return jax.nn.gelu(x, approximate=True)

def _silu(x):
    return jax.nn.silu(x)

def _sigmoid(x):
    return jax.nn.sigmoid(x)

def _layernorm(x, axis=-1, eps=1e-05):
    m = jnp.mean(x, axis=axis, keepdims=True)
    v = jnp.var(x, axis=axis, keepdims=True)
    return (x - m) / jnp.sqrt(v + eps)

def _scatter_add(tgt, idx, src, axis=0):
    return tgt.at[idx].add(src)

def _segment_sum(src, seg, n):
    return jax.ops.segment_sum(src, seg, n)
kernel_name = 'mk_xattn_seq_d2_seqx_r8_f164f6'

def setup_inputs(seed: int=0):
    np.random.seed(seed)
    _w = jnp.asarray

    def _rec_inputs():
        import jax
        import jax.numpy as jnp
        _rk = jax.random.key(seed)
        x = -0.0001233 + 1 * jax.random.normal(jax.random.fold_in(_rk, 1), (8, 256, 160), jnp.float32)
        _lenS = 256 - jax.random.randint(jax.random.fold_in(_rk, 7), (8,), 0, max(1, 256 // 4) + 1, jnp.int32)
        _lenS2 = 512 - jax.random.randint(jax.random.fold_in(_rk, 8), (8,), 0, max(1, 512 // 4) + 1, jnp.int32)
        _ctx_768P = jax.random.normal(jax.random.fold_in(_rk, 11), (8, 16, 96), jnp.float32)
        _ctx_768c = jax.random.dirichlet(jax.random.fold_in(_rk, 511), 0.3 * jnp.ones((16,), jnp.float32), (8, 512))
        _ctx_768t = jnp.einsum('bsk,bkd->bsd', _ctx_768c, _ctx_768P)
        _ctx_768t = _ctx_768t * jax.lax.rsqrt(jnp.mean(jnp.square(_ctx_768t)) + 1e-12) * 0.953939
        ctx_768 = 0.00272024 + 0.999456 * (_ctx_768t + 0.3 * jax.random.normal(jax.random.fold_in(_rk, 611), (8, 512, 96), jnp.float32))
        return (x, ctx_768)
    x, ctx_768 = _rec_inputs()

    def _L0_xattn_setup():
        import jax, jax.numpy as jnp
        import numpy as np
        D = 160
        H = 20
        DH = D // H
        CTX = 96
        FF_IN = 4 * D
        EPS = 1e-05

        def _ln(x, g, b):
            m = jnp.mean(x, axis=-1, keepdims=True)
            v = jnp.mean(jnp.square(x - m), axis=-1, keepdims=True)
            return (x - m) * jax.lax.rsqrt(v + EPS) * g + b

        def _attn(x, ctx, wq, wk, wv, wo, bo, heads):
            b, n, _ = x.shape
            j = ctx.shape[1]
            dh = wq.shape[1] // heads
            scale = dh ** (-0.5)
            q = (x @ wq).reshape(b, n, heads, dh).transpose(0, 2, 1, 3)
            k = (ctx @ wk).reshape(b, j, heads, dh).transpose(0, 2, 1, 3)
            v = (ctx @ wv).reshape(b, j, heads, dh).transpose(0, 2, 1, 3)
            sim = jnp.einsum('bhid,bhjd->bhij', q, k) * scale
            a = jax.nn.softmax(sim, axis=-1)
            out = jnp.einsum('bhij,bhjd->bhid', a, v)
            out = out.transpose(0, 2, 1, 3).reshape(b, n, heads * dh)
            return out @ wo + bo
        key = jax.random.key(seed)
        ks = jax.random.split(key, 24)
        r = lambda k, shp, s: jax.random.normal(k, shp, dtype=jnp.float32) * s
        d = {'x': r(ks[0], (8, 128, D), 1.0), 'context': r(ks[1], (8, 77, CTX), 1.0), 'heads': H, 'n1_g': jnp.ones((D,), jnp.float32), 'n1_b': jnp.zeros((D,), jnp.float32), 'q1': r(ks[2], (D, D), D ** (-0.5)), 'k1': r(ks[3], (D, D), D ** (-0.5)), 'v1': r(ks[4], (D, D), D ** (-0.5)), 'o1_w': r(ks[5], (D, D), D ** (-0.5)), 'o1_b': jnp.zeros((D,), jnp.float32), 'n2_g': jnp.ones((D,), jnp.float32), 'n2_b': jnp.zeros((D,), jnp.float32), 'q2': r(ks[6], (D, D), D ** (-0.5)), 'k2': r(ks[7], (CTX, D), CTX ** (-0.5)), 'v2': r(ks[8], (CTX, D), CTX ** (-0.5)), 'o2_w': r(ks[9], (D, D), D ** (-0.5)), 'o2_b': jnp.zeros((D,), jnp.float32), 'n3_g': jnp.ones((D,), jnp.float32), 'n3_b': jnp.zeros((D,), jnp.float32), 'ff_w1': r(ks[10], (D, 2 * FF_IN), D ** (-0.5)), 'ff_b1': jnp.zeros((2 * FF_IN,), jnp.float32), 'ff_w2': r(ks[11], (FF_IN, D), FF_IN ** (-0.5)), 'ff_b2': jnp.zeros((D,), jnp.float32)}
        return d
    _L0_xattn_all = _L0_xattn_setup()
    _L0_xattn_in = {k: v for k, v in _L0_xattn_all.items() if k in ('n1_g', 'n1_b', 'q1', 'k1', 'v1', 'o1_w', 'o1_b', 'n2_g', 'n2_b', 'q2', 'k2', 'v2', 'o2_w', 'o2_b', 'n3_g', 'n3_b', 'ff_w1', 'ff_b1', 'ff_w2', 'ff_b2')}
    del _L0_xattn_all

    def _L1_xattn_setup():
        import jax, jax.numpy as jnp
        import numpy as np
        HEADS = 8
        NUM_TOKENS = 4
        CROSS_ATTENTION_DIM = 96

        def _mha(q, k, v, heads=HEADS):
            B, Sq, H = q.shape
            Sk = k.shape[1]
            d = H // heads
            qh = q.reshape(B, Sq, heads, d).transpose(0, 2, 1, 3)
            kh = k.reshape(B, Sk, heads, d).transpose(0, 2, 1, 3)
            vh = v.reshape(B, Sk, heads, d).transpose(0, 2, 1, 3)
            scores = jnp.einsum('bhqd,bhkd->bhqk', qh, kh) * jnp.asarray(d, q.dtype) ** (-0.5)
            probs = jax.nn.softmax(scores, axis=-1)
            out = jnp.einsum('bhqk,bhkd->bhqd', probs, vh)
            return out.transpose(0, 2, 1, 3).reshape(B, Sq, H)
        key = jax.random.key(seed)
        ks = jax.random.split(key, 10)
        B, S, H, CAD, T = (4, 128, 160, CROSS_ATTENTION_DIM, NUM_TOKENS)
        sc = 0.02
        return {'hidden_states': jax.random.normal(ks[0], (B, S, H), jnp.float32), 'encoder_hidden_states': jax.random.normal(ks[1], (B, 77 + T, CAD), jnp.float32), 'Wq': jax.random.normal(ks[2], (H, H), jnp.float32) * sc, 'Wk': jax.random.normal(ks[3], (CAD, H), jnp.float32) * sc, 'Wv': jax.random.normal(ks[4], (CAD, H), jnp.float32) * sc, 'Wq_ca': jax.random.normal(ks[5], (T, H), jnp.float32) * sc, 'Wk_ca': jax.random.normal(ks[6], (CAD, H), jnp.float32) * sc, 'Wv_ca': jax.random.normal(ks[7], (CAD, H), jnp.float32) * sc, 'Wout': jax.random.normal(ks[8], (H, H), jnp.float32) * sc, 'b_out': jnp.zeros((H,), jnp.float32)}
    _L1_xattn_all = _L1_xattn_setup()
    _L1_xattn_in = {k: v for k, v in _L1_xattn_all.items() if k in ('Wq', 'Wk', 'Wv', 'Wq_ca', 'Wk_ca', 'Wv_ca', 'Wout', 'b_out')}
    del _L1_xattn_all
    return {'x': x, 'ctx_768': ctx_768, 'L0_xattn_n1_g': _L0_xattn_in['n1_g'], 'L0_xattn_n1_b': _L0_xattn_in['n1_b'], 'L0_xattn_q1': _L0_xattn_in['q1'], 'L0_xattn_k1': _L0_xattn_in['k1'], 'L0_xattn_v1': _L0_xattn_in['v1'], 'L0_xattn_o1_w': _L0_xattn_in['o1_w'], 'L0_xattn_o1_b': _L0_xattn_in['o1_b'], 'L0_xattn_n2_g': _L0_xattn_in['n2_g'], 'L0_xattn_n2_b': _L0_xattn_in['n2_b'], 'L0_xattn_q2': _L0_xattn_in['q2'], 'L0_xattn_k2': _L0_xattn_in['k2'], 'L0_xattn_v2': _L0_xattn_in['v2'], 'L0_xattn_o2_w': _L0_xattn_in['o2_w'], 'L0_xattn_o2_b': _L0_xattn_in['o2_b'], 'L0_xattn_n3_g': _L0_xattn_in['n3_g'], 'L0_xattn_n3_b': _L0_xattn_in['n3_b'], 'L0_xattn_ff_w1': _L0_xattn_in['ff_w1'], 'L0_xattn_ff_b1': _L0_xattn_in['ff_b1'], 'L0_xattn_ff_w2': _L0_xattn_in['ff_w2'], 'L0_xattn_ff_b2': _L0_xattn_in['ff_b2'], 'L1_xattn_Wq': _L1_xattn_in['Wq'], 'L1_xattn_Wk': _L1_xattn_in['Wk'], 'L1_xattn_Wv': _L1_xattn_in['Wv'], 'L1_xattn_Wq_ca': _L1_xattn_in['Wq_ca'], 'L1_xattn_Wk_ca': _L1_xattn_in['Wk_ca'], 'L1_xattn_Wv_ca': _L1_xattn_in['Wv_ca'], 'L1_xattn_Wout': _L1_xattn_in['Wout'], 'L1_xattn_b_out': _L1_xattn_in['b_out']}

def reference(x, ctx_768, L0_xattn_n1_g, L0_xattn_n1_b, L0_xattn_q1, L0_xattn_k1, L0_xattn_v1, L0_xattn_o1_w, L0_xattn_o1_b, L0_xattn_n2_g, L0_xattn_n2_b, L0_xattn_q2, L0_xattn_k2, L0_xattn_v2, L0_xattn_o2_w, L0_xattn_o2_b, L0_xattn_n3_g, L0_xattn_n3_b, L0_xattn_ff_w1, L0_xattn_ff_b1, L0_xattn_ff_w2, L0_xattn_ff_b2, L1_xattn_Wq, L1_xattn_Wk, L1_xattn_Wv, L1_xattn_Wq_ca, L1_xattn_Wk_ca, L1_xattn_Wv_ca, L1_xattn_Wout, L1_xattn_b_out):
    import jax
    import jax.numpy as jnp

    def _L0_xattn_ref(x, context, heads, n1_g, n1_b, q1, k1, v1, o1_w, o1_b, n2_g, n2_b, q2, k2, v2, o2_w, o2_b, n3_g, n3_b, ff_w1, ff_b1, ff_w2, ff_b2):
        import jax, jax.numpy as jnp
        import numpy as np
        D = 160
        H = 20
        DH = D // H
        CTX = 96
        FF_IN = 4 * D
        EPS = 1e-05

        def _ln(x, g, b):
            m = jnp.mean(x, axis=-1, keepdims=True)
            v = jnp.mean(jnp.square(x - m), axis=-1, keepdims=True)
            return (x - m) * jax.lax.rsqrt(v + EPS) * g + b

        def _attn(x, ctx, wq, wk, wv, wo, bo, heads):
            b, n, _ = x.shape
            j = ctx.shape[1]
            dh = wq.shape[1] // heads
            scale = dh ** (-0.5)
            q = (x @ wq).reshape(b, n, heads, dh).transpose(0, 2, 1, 3)
            k = (ctx @ wk).reshape(b, j, heads, dh).transpose(0, 2, 1, 3)
            v = (ctx @ wv).reshape(b, j, heads, dh).transpose(0, 2, 1, 3)
            sim = jnp.einsum('bhid,bhjd->bhij', q, k) * scale
            a = jax.nn.softmax(sim, axis=-1)
            out = jnp.einsum('bhij,bhjd->bhid', a, v)
            out = out.transpose(0, 2, 1, 3).reshape(b, n, heads * dh)
            return out @ wo + bo
        h1 = _ln(x, n1_g, n1_b)
        x = _attn(h1, h1, q1, k1, v1, o1_w, o1_b, heads) + x
        h2 = _ln(x, n2_g, n2_b)
        x = _attn(h2, context, q2, k2, v2, o2_w, o2_b, heads) + x
        h3 = _ln(x, n3_g, n3_b)
        proj = h3 @ ff_w1 + ff_b1
        a, g = jnp.split(proj, 2, axis=-1)
        ff = a * jax.nn.gelu(g, approximate=False) @ ff_w2 + ff_b2
        return ff + x

    def _L1_xattn_ref(hidden_states, encoder_hidden_states, Wq, Wk, Wv, Wq_ca, Wk_ca, Wv_ca, Wout, b_out):
        import jax, jax.numpy as jnp
        import numpy as np
        HEADS = 8
        NUM_TOKENS = 4
        CROSS_ATTENTION_DIM = 96

        def _mha(q, k, v, heads=HEADS):
            B, Sq, H = q.shape
            Sk = k.shape[1]
            d = H // heads
            qh = q.reshape(B, Sq, heads, d).transpose(0, 2, 1, 3)
            kh = k.reshape(B, Sk, heads, d).transpose(0, 2, 1, 3)
            vh = v.reshape(B, Sk, heads, d).transpose(0, 2, 1, 3)
            scores = jnp.einsum('bhqd,bhkd->bhqk', qh, kh) * jnp.asarray(d, q.dtype) ** (-0.5)
            probs = jax.nn.softmax(scores, axis=-1)
            out = jnp.einsum('bhqk,bhkd->bhqd', probs, vh)
            return out.transpose(0, 2, 1, 3).reshape(B, Sq, H)
        residual = hidden_states
        unet_size = residual.shape[1]
        end_pos = encoder_hidden_states.shape[1] - NUM_TOKENS
        enc = encoder_hidden_states[:, :end_pos, :]
        ca = encoder_hidden_states[:, end_pos:, :]
        query = hidden_states @ Wq
        keyt = enc @ Wk
        valt = enc @ Wv
        hs = _mha(query, keyt, valt)
        ca_q1 = jnp.einsum('btc,th->bch', ca, Wq_ca)
        indices = np.linspace(0, CROSS_ATTENTION_DIM - 1, unet_size).astype(np.int64)
        ca_q1 = ca_q1[:, indices, :]
        ca_hs1 = _mha(ca_q1, residual, residual)
        ca_q2 = ca_hs1 @ Wq
        ca_k2 = ca @ Wk_ca
        ca_v2 = ca @ Wv_ca
        ca_hs2 = _mha(ca_q2, ca_k2, ca_v2)
        out = hs + ca_hs2
        out = out @ Wout + b_out
        out = out + residual
        return out
    x = _L0_xattn_ref(x, ctx_768, 20, L0_xattn_n1_g, L0_xattn_n1_b, L0_xattn_q1, L0_xattn_k1, L0_xattn_v1, L0_xattn_o1_w, L0_xattn_o1_b, L0_xattn_n2_g, L0_xattn_n2_b, L0_xattn_q2, L0_xattn_k2, L0_xattn_v2, L0_xattn_o2_w, L0_xattn_o2_b, L0_xattn_n3_g, L0_xattn_n3_b, L0_xattn_ff_w1, L0_xattn_ff_b1, L0_xattn_ff_w2, L0_xattn_ff_b2)
    x = _L1_xattn_ref(x, ctx_768, L1_xattn_Wq, L1_xattn_Wk, L1_xattn_Wv, L1_xattn_Wq_ca, L1_xattn_Wk_ca, L1_xattn_Wv_ca, L1_xattn_Wout, L1_xattn_b_out)
    return x

_drawn_inputs = setup_inputs


def setup_inputs(seed=0):
    import zlib

    import numpy as np

    out = dict(_drawn_inputs(seed))
    spreads = {'L0_xattn_n1_g': (1.0, 0.2),
     'L0_xattn_n1_b': (0.0, 0.1),
     'L0_xattn_o1_b': (0.0, 0.1),
     'L0_xattn_n2_g': (1.0, 0.2),
     'L0_xattn_n2_b': (0.0, 0.371),
     'L0_xattn_o2_b': (0.0, 0.1),
     'L0_xattn_n3_g': (1.0, 0.2),
     'L0_xattn_n3_b': (0.0, 0.1),
     'L0_xattn_ff_b1': (0.0, 0.1),
     'L0_xattn_ff_b2': (0.0, 0.1),
     'L1_xattn_b_out': (0.0, 0.1)}
    factors = {'L1_xattn_Wq': 8.0,
     'L1_xattn_Wk': 8.0,
     'L1_xattn_Wv': 3.162,
     'L1_xattn_Wq_ca': 172.637,
     'L1_xattn_Wk_ca': 30.484}
    for name, (base, spread) in spreads.items():
        noise = np.random.default_rng([zlib.crc32(name.encode()), seed]).standard_normal(out[name].shape)
        drawn = base * np.exp(spread * noise) if base else spread * noise
        out[name] = jnp.asarray(drawn.astype(out[name].dtype))
    for name, factor in factors.items():
        out[name] = (out[name] * factor).astype(out[name].dtype)
    return out
```

```python
from contextlib import ExitStack

import concourse.bass as bass
from concourse import mybir

ALU = mybir.AluOpType
ACT = mybir.ActivationFunctionType
F32 = mybir.dt.float32
BF16 = mybir.dt.bfloat16
X = mybir.AxisListType.X

B, N, D = 8, 256, 160
J, CD = 512, 96
FF = 4 * D
CA = 4
NQA = CD
HALF = D // 2
TT = N // 128
JT = J // 128
EPS = 1e-5
STREAMS = 2
READY0 = 1 + 2 + 1 + 4 + 11 + 2
PAIRS = B // STREAMS
GH = 4
HW = 32
P_RING = 2
ST_BANKS = 3
MX_BANKS = 2


class Family:

    def __init__(self, name, heads, dh, nq, nk, buffer_keys):
        self.name, self.heads, self.dh, self.nq, self.nk = name, heads, dh, nq, nk
        self.buffer_keys = buffer_keys
        self.groups = heads // GH
        self.q_tiles = [(t, min(128, nq - t)) for t in range(0, nq, 128)]
        self.k_tiles = [min(128, nk - t) for t in range(0, nk, 128)]
        self.pairs = len(self.k_tiles) // 2
        self.per_bank = 512 // nk
        self.fills = GH * len(self.q_tiles) // self.per_bank
        self.scale = float(dh) ** -0.5
        self.m_row = 96 if dh == 8 else 6 * dh
        self.max_rows = self.m_row
        self.st_rows = 128 if dh == 8 else self.m_row + 2


SELF = Family("self", 20, 8, N, N, J)
CROSS = Family("cross", 20, 8, N, J, J)
TEXT = Family("text", 8, 20, N, J - CA, J)
CAM = Family("cam", 8, 20, NQA, N, N)
FAMILIES = [SELF, CROSS, TEXT, CAM]
Q_PARTS = (0, 0, 0, 1, 1, 2)
K_PARTS = (0, 1, 2, 0, 1, 0)
ROW_LOADS = ((0, 3, 0), (3, 2, 1), (5, 1, 2))

MISC_USES = {
    "ctxT": "A", "lnT": "A", "q": "D", "k": "D", "kctx": "DD", "v": "A", "vctx": "AA",
    "outT": "A", "out": "D", "ff1": "DDDDD", "ff2": "D", "xT": "D", "camq": "D", "cambc": "AAAA",
    "cam2T": "A", "cam2q": "A", "hsumT": "A", "fin": "D", "MT": "A", "EVT": "D",
}


SPLIT_STEPS = ("q", "k", "kctx", "camq", "xT")
DVE_LINKS = {"ln": 2, "NM": 1, "EVT": 1, "cam2": 4}
N_WEIGHT_LOADS = 9 + 6 + 1 + 2 + 2 + 1 + 6 + 4
WEIGHTS = {
    "q1": "L0_xattn_q1", "k1": "L0_xattn_k1", "v1": "L0_xattn_v1", "o1": "L0_xattn_o1_w", "o1_b": "L0_xattn_o1_b",
    "q2": "L0_xattn_q2", "k2": "L0_xattn_k2", "v2": "L0_xattn_v2", "o2": "L0_xattn_o2_w", "o2_b": "L0_xattn_o2_b",
    "n1_g": "L0_xattn_n1_g", "n1_b": "L0_xattn_n1_b", "n2_g": "L0_xattn_n2_g", "n2_b": "L0_xattn_n2_b",
    "n3_g": "L0_xattn_n3_g", "n3_b": "L0_xattn_n3_b",
    "ff_w1": "L0_xattn_ff_w1", "ff_b1": "L0_xattn_ff_b1", "ff_w2": "L0_xattn_ff_w2", "ff_b2": "L0_xattn_ff_b2",
    "Wq": "L1_xattn_Wq", "Wk": "L1_xattn_Wk", "Wv": "L1_xattn_Wv", "Wq_ca": "L1_xattn_Wq_ca",
    "Wk_ca": "L1_xattn_Wk_ca", "Wv_ca": "L1_xattn_Wv_ca", "Wout": "L1_xattn_Wout", "b_out": "L1_xattn_b_out",
}


def make_schedule():
    steps, uses = [], []

    def add(name, *args):
        steps.append((name, args, len(uses)))
        uses.extend(MISC_USES.get(name, ""))

    seq = [(f, s, g) for f, s in ((SELF, 0), (SELF, 1), (CROSS, 0), (CROSS, 1))
           for g in range(f.groups)]
    seq += [(f, s, g) for s in range(2) for f in (TEXT, CAM) for g in range(f.groups)]
    units = [(n, p) for n, (f, s, g) in enumerate(seq) for p in range(f.pairs)]

    def pre_self(s):
        return [("ln", 0, s), ("zeros", s), ("lnT", 0, s), ("k", SELF, s), ("q", SELF, s),
                ("v", SELF, s), ("spreadk", SELF, s), ("spreadq", SELF, s), ("ctxT", s)]

    def mid_cross(s):
        return [("kctx", CROSS, s), ("outT", SELF, s), ("spreadk", CROSS, s), ("out", SELF, s), ("ln", 1, s),
                ("vctx", CROSS, s), ("lnT", 1, s), ("q", CROSS, s), ("spreadq", CROSS, s)]

    def mid_last(s):
        return [("outT", CROSS, s), ("ones", s), ("out", CROSS, s), ("ln", 2, s), ("kctx", TEXT, s), ("vctx", TEXT, s),
                ("lnT", 2, s), ("spreadk", TEXT, s), ("ff1", s), ("camq", s), ("gelu", s), ("ff2", s),
                ("xT", s), ("q", TEXT, s), ("spreadq", TEXT, s), ("spreadk", CAM, s), ("spreadq", CAM, s)]

    def end(s):
        return [("cambc", s), ("cam2T", s), ("cam2q", s), ("cam2", s), ("hsumT", s), ("fin", s)]

    first = {}
    for n, (f, s, g) in enumerate(seq):
        first.setdefault((f.name, s), n)
    chains = {first["self", 1]: mid_cross(0), first["cross", 0]: mid_cross(1),
              first["cross", 1]: mid_last(0), first["text", 0]: mid_last(1),
              first["text", 1]: end(0)}
    need = {first["self", 1]: first["cross", 0] - 2, first["cross", 0]: first["cross", 1] - 2,
            first["cross", 1]: first["text", 0] - 2, first["text", 0]: first["text", 1] - 2,
            first["text", 1]: len(seq)}

    for s in range(2):
        add("load", s)
    for s in range(2):
        for st in pre_self(s):
            add(*st)

    fill = {}

    def fills(n, upto):
        f = seq[n][0]
        while fill.get(n, 0) < upto:
            k = fill.get(n, 0)
            add("MX", n, k)
            fill[n] = k + 1
            if k + 1 == f.fills:
                add("NM", n)

    fills(0, seq[0][0].fills)
    fills(1, seq[1][0].fills)
    add("MT", 0)
    pending, when = [], 0
    evt = []
    for u, (n, p) in enumerate(units):
        f = seq[n][0]
        if p == 0 and n in chains:
            assert not pending, (n, pending)
            pending, when = list(chains[n]), need[n]
            wait_units = 2
        todo = [c for c in evt]
        for k in range(GH):
            add("ST", n, p, u, k)
            if n + 2 < len(seq):
                f2 = seq[n + 2][0]
                if pending and n + 2 >= when + 2:
                    while pending:
                        add(*pending.pop(0))
                fills(n + 2, f2.fills * (p * GH + k + 1) // (f.pairs * GH))
            if k == 1 and p == 0 and n + 1 < len(seq):
                add("MT", n + 1)
            if k == 2:
                for c in todo:
                    add("EVT", c)
                    evt.remove(c)
        if u:
            add("PV", *units[u - 1], u - 1)
            pn, pp = units[u - 1]
            if pp == seq[pn][0].pairs - 1:
                add("EVC", pn, u - 1)
                evt.append(pn)
        if pending:
            if wait_units:
                wait_units -= 1
            else:
                left = max(1, sum(1 for m, _ in units[u:] if m < when))
                for _ in range(-(-len(pending) // left)):
                    add(*pending.pop(0))
    while pending:
        add(*pending.pop(0))
    add("PV", *units[-1], len(units) - 1)
    add("EVC", units[-1][0], len(units) - 1)
    evt.append(units[-1][0])
    for c in evt:
        add("EVT", c)
    for st in end(1):
        add(*st)
    return steps, uses, seq, units


def two_blocks(nc, x, ctx, w, out):
    steps, uses, seq, units = make_schedule()
    ordinal = [uses[:m + 1].count(u) for m, u in enumerate(uses)]
    fill_no = {}
    for name, args, _ in steps:
        if name == "MX":
            fill_no[args] = len(fill_no)
    use_no = {(nm,) + tuple(a.name if isinstance(a, Family) else a for a in args): m
              for nm, args, m in steps if nm in MISC_USES}
    turn_use = {args[0]: m for name, args, m in steps if name == "MT"}

    with ExitStack() as stack:
        def sb(name, shape, dt=F32):
            return stack.enter_context(nc.sbuf_tensor(name, shape, dt))

        def per_stream(name, shape, dt=F32):
            return [sb(f"{name}_{s}", shape, dt) for s in range(STREAMS)]

        def sem(name):
            return stack.enter_context(nc.semaphore(name))

        mx_bank = [stack.enter_context(nc.psum_tensor(f"mx_bank{i}", [128, 512], F32)) for i in range(MX_BANKS)]
        st_bank = [stack.enter_context(nc.psum_tensor(f"st_bank{i}", [128, 512], F32)) for i in range(ST_BANKS)]
        o_bank = stack.enter_context(nc.psum_tensor("o_bank", [128, 512], F32))
        misc = [stack.enter_context(nc.psum_tensor(f"misc{i}", [128, 512], F32)) for i in range(2)]

        wide = {n: sb("w_" + n, [HALF, 2, D]) for n in ("q1", "k1", "v1", "o1", "q2", "o2", "Wq", "Wout")}
        thin = {n: sb("w_" + n, [CD, D]) for n in ("k2", "v2", "Wk", "Wv", "Wk_ca", "Wv_ca")}
        w_qca = sb("w_qca", [CA, D])
        w_ff1 = sb("w_ff1", [HALF, 2, 2 * FF])
        w_ff2 = sb("w_ff2", [128, FF // 128, D])
        b_ff1 = sb("b_ff1", [128, 2 * FF // 128])
        gains = sb("gains", [HALF, 3, 2])
        shifts = sb("shifts", [HALF, 3, 2])
        biases = {n: sb("b_" + n, [128, D]) for n in ("o1", "o2", "ff2", "out")}
        by_row = [(wide["q1"], SELF), (wide["k1"], SELF), (wide["q2"], CROSS), (wide["Wq"], TEXT),
                  (thin["k2"], CROSS), (thin["Wk"], TEXT), (w_qca, CAM)]
        ident = sb("ident", [128, 128])
        ident_bf = sb("ident_bf", [128, 128], BF16)
        pick = sb("pick", [NQA, N])
        minus_half = sb("minus_half", [128, TT])

        x_sb = per_stream("x_sb", [128, TT, D])
        xb_sb = per_stream("xb_sb", [128, TT, D])
        ca_sb = per_stream("ca_sb", [CA, CD])
        ctxT = per_stream("ctxT", [CD, J])
        xn = per_stream("xn", [128, TT, D])
        hT = per_stream("hT", [HALF, 2, N])
        stats = per_stream("stats", [128, TT, 6])
        mean_var = per_stream("mean_var", [128, TT, 2])
        var_eps = per_stream("var_eps", [128, TT])
        rstd = per_stream("rstd", [128, TT])
        q8, k8 = per_stream("q8", [128, 20, N], BF16), per_stream("k8", [128, 20, J], BF16)
        v8 = per_stream("v8", [128, JT, 20, HW])
        qt_ = [a[:, 0:8, :] for a in q8]
        kt_ = [a[:, 0:8, :] for a in k8]
        qc_ = [a[:, 8:11, :].rearrange("p a b -> p (a b)").rearrange("p (h t) -> p h t", h=8) for a in q8]
        kc_ = [a[:, 8:12, :].rearrange("p a b -> p (a b)").rearrange("p (h t) -> p h t", h=8) for a in k8]
        vt_ = [a[:, :, 0:8, :] for a in v8]
        vc_ = [a[:, 0:TT, 8:16, :] for a in v8]
        q_rows = {"self": q8, "cross": q8, "text": qt_, "cam": qc_}
        k_rows = {"self": k8, "cross": k8, "text": kt_, "cam": kc_}
        v_rows = {"self": v8, "cross": v8, "text": vt_, "cam": vc_}
        o_tok = per_stream("o_tok", [128, TT, D])
        o_cam = [sb("o_cam", [NQA, 1, D])] * STREAMS
        turned = per_stream("turned", [128, 2 * N])
        oT = [a[0:HALF, :].rearrange("p (c t) -> p c t", c=2) for a in turned]
        ctx_sb = [a[:, 0:JT * CD].rearrange("p (t d) -> p t d", t=JT) for a in turned]
        q_parts = per_stream("q_parts", [HALF, 3, 2, N], BF16)
        k_parts = per_stream("k_parts", [HALF, 3, 2, J], BF16)
        cq_parts = per_stream("cq_parts", [HALF, 3, 2, NQA], BF16)
        ck_parts = per_stream("ck_parts", [HALF, 3, 2, N], BF16)
        ca_wide = per_stream("ca_wide", [CD, CA, NQA])
        y_sb = xn
        cam_out = [sb("cam_out", [NQA, D])] * STREAMS

        rest = [sb(f"rest{i}", [HALF, 512]) for i in range(2)]
        probs = sb("probs", [128, P_RING, GH, 512])
        neg_max = [sb(f"neg_max{i}", [128, GH * TT]) for i in range(2)]
        m_parts = [sb(f"m_parts{i}", [128, TT, 2, GH], BF16) for i in range(2)]
        mT = [sb(f"mT{i}", [2 * GH, N], BF16) for i in range(2)]
        o_sb = [sb(f"o_sb{i}", [128, N]) for i in range(2)]
        recip = [sb(f"recip{i}", [128, TT, GH]) for i in range(2)]
        ff_a = sb("ff_a", [128, FF // 128, N])
        ff_g = sb("ff_g", [128, FF // 128, N])
        kb = sb("kb", [NQA, CA, D])
        vb = sb("vb", [NQA, CA, D])
        cam_q = sb("cam_q", [NQA, D])
        cam_t = sb("cam_t", [NQA, CA, D])
        cam_s = sb("cam_s", [NQA, CA, 8])
        cam_m = sb("cam_m", [NQA, 8])
        cam_d = sb("cam_d", [NQA, CA, 8])
        cam_e = sb("cam_e", [NQA, CA, 8])
        cam_z = sb("cam_z", [NQA, 8])

        raw, place = {}, 0
        for wt, f in by_row:
            shape = list(wt.shape)
            size = shape[1] * shape[2] if len(shape) == 3 else shape[1]
            raw[wt.name] = probs[0:shape[0], :, :, :].rearrange("p a b c -> p (a b c)")[:, place:place + size]
            place += size

        def scratch(name, cols):
            return [nc.dram_tensor(f"{name}_{s}", [3, D, cols], BF16, kind="Internal").ap() for s in range(STREAMS)]

        q_scr = {f.name: scratch("qs_" + f.name, f.nq) for f in FAMILIES}
        k_scr = {f.name: scratch("ks_" + f.name, N if f in (SELF, CAM) else J) for f in FAMILIES}
        parts_q = {"self": q_parts, "cross": q_parts, "text": q_parts, "cam": cq_parts}
        parts_k = {"self": k_parts, "cross": k_parts, "text": k_parts, "cam": ck_parts}

        w_in = sem("w_in")
        ready0 = sem("ready0")
        x_in = [sem(f"x_in{s}") for s in range(2)]
        c_in = [sem(f"c_in{s}") for s in range(2)]
        misc_full = sem("misc_full")
        misc_taken = {"A": sem("misc_taken_act"), "D": sem("misc_taken_dve")}
        mx_full, mx_read = sem("mx_full"), sem("mx_read")
        m_split = sem("m_split")
        m_in = [sem(f"m_in{i}") for i in range(2)]
        st_full, exp_done = sem("st_full"), sem("exp_done")
        pv_done, o_read = sem("pv_done"), sem("o_read")
        hi_done = sem("hi_done")
        split_done = sem("split_done")
        parts_out = {(a, f.name): [sem(f"{a}_out_{f.name}{s}") for s in range(2)] for a in "qk" for f in FAMILIES}
        rows_in = {f.name: [sem(f"rows_in_{f.name}{s}") for s in range(2)] for f in FAMILIES}
        var_done, rstd_done, xn_done = sem("var_done"), sem("rstd_done"), sem("xn_done")
        xh_done, xb_done, x_by_row = sem("xh_done"), sem("xb_done"), sem("x_by_row")
        zeros_done = sem("zeros_done")
        ones_done = sem("ones_done")
        wide_done, cv_done = sem("wide_done"), sem("cv_done")
        gate_done, gelu_done, ff_done = sem("gate_done"), sem("gelu_done"), sem("ff_done")
        cam_prod, cam_arg, cam_exp, cam_p = (sem(n) for n in ("cam_prod", "cam_arg", "cam_exp", "cam_p"))
        cam_pv, cam_done = sem("cam_pv"), sem("cam_done")
        dve_step, pool_step, zero_step = sem("dve_step"), sem("pool_step"), sem("zero_step")
        passed = sem("passed")
        y_out = sem("y_out")

        n_groups, n_units = len(seq), len(units)
        splits = [(name, args, m) for name, args, m in steps if name in SPLIT_STEPS]
        split_no, c = {}, 0
        for name, args, m in splits:
            split_no[m] = c
            c += len(MISC_USES[name])
        n_splits = c
        total = {}
        order = {}

        def count(s, keys, by=1):
            total[s.name] = by * len(keys)
            for i, k in enumerate(keys):
                order[s.name, k] = by * (i + 1)

        def of(*names):
            return [(nm,) + tuple(a.name if isinstance(a, Family) else a for a in args)
                    for nm, args, _ in steps if nm in names]

        count(misc_full, list(range(len(uses))))
        for e in "AD":
            count(misc_taken[e], [m for m, u in enumerate(uses) if u == e])
        count(mx_full, list(range(len(fill_no))))
        count(mx_read, list(range(len(fill_no))))
        for s in (o_read,):
            count(s, list(range(n_groups)))
        count(m_split, [a[0] for nm, a, _ in steps if nm == "NM"])
        for par in range(2):
            count(m_in[par], list(range(par, n_groups, 2)), 16)
        count(st_full, list(range(4 * n_units)))
        count(exp_done, list(range(4 * n_units)))
        count(pv_done, list(range(n_units)))
        for s in (hi_done, split_done):
            count(s, list(range(n_splits)))
        for f in FAMILIES:
            for s in range(2):
                count(rows_in[f.name][s], [0], 16 * 2 * len(ROW_LOADS))
                for a in "qk":
                    count(parts_out[a, f.name][s], [0], 16 * 2)
        for s in (var_done, rstd_done, xn_done):
            count(s, of("ln"))
        count(xh_done, of("xT"))
        count(x_by_row, of("ff2"))
        count(xb_done, [k for k in of("ln", "xT")])
        count(wide_done, of("ctxT"))
        count(zeros_done, of("zeros"))
        count(ones_done, of("ones"))
        total[zero_step.name] = len(of("zeros"))
        count(cv_done, of("xT"))
        for s_ in (gate_done,):
            count(s_, [("ff1", s, j) for s in range(2) for j in range(FF // 128)])
        count(gelu_done, of("gelu"))
        count(ff_done, of("gelu"))
        for s in (cam_prod, cam_arg, cam_exp, cam_p, cam_pv, cam_done):
            count(s, of("cam2"))
        count(y_out, of("fin"), 16)
        for s in range(2):
            count(x_in[s], [0], 16)
            count(c_in[s], [0], 32)
        total[dve_step.name] = sum(DVE_LINKS.get(name, 0) for name, _, _ in steps)

        last_group = {}
        for n, (f, s, g) in enumerate(seq):
            last_group[f.name, s] = n

        def split_views(name, args, m, o):
            s = args[-1]
            bank = misc[(m + o) % 2][0:HALF, :]
            if name == "kctx":
                return [k_parts[s][:, p, o, :] for p in range(3)], bank
            bank = bank.rearrange("p (c t) -> p c t", c=2)
            if name == "camq":
                return [cq_parts[s][:, p, :, :] for p in range(3)], bank[:, :, 0:NQA]
            if name == "xT":
                return [ck_parts[s][:, p, :, :] for p in range(3)], bank
            if name == "q":
                return [q_parts[s][:, p, :, :] for p in range(3)], bank
            return [k_parts[s][:, p, :, 0:N] for p in range(3)], bank

        def rest_view(no, like):
            shape = list(like.shape)
            if len(shape) == 2:
                return rest[no % 2][:, :]
            return rest[no % 2][:, :].rearrange("p (c t) -> p c t", c=2)[:, :, 0:shape[2]]

        block = stack.enter_context(nc.Block())

        @block.sync
        def _(sp):
            loads = 0

            def fetch(dst, src):
                nonlocal loads
                sp.dma_start(dst, src).then_inc(w_in, 16)
                loads += 1

            def as_loaded(wt):
                if wt.name not in raw:
                    return wt
                return raw[wt.name].rearrange("p (c n) -> p c n", n=D) if len(wt.shape) == 3 else raw[wt.name]

            for n in wide:
                if n == "Wq":
                    for c in range(2):
                        fetch(as_loaded(wide[n])[:, c, :], w[n].rearrange("(h r) n -> r h n", h=CAM.heads)[c * CAM.dh // 2:(c + 1) * CAM.dh // 2, :, :])
                else:
                    fetch(as_loaded(wide[n])[:, :, :], w[n].rearrange("(c p) n -> p c n", c=2))
            for n in thin:
                fetch(as_loaded(thin[n])[:, :], w[n])
            fetch(as_loaded(w_qca)[:, :], w["Wq_ca"])
            fetch(w_ff1[:, :, :], w["ff_w1"].rearrange("(c p) n -> p c n", c=2))
            fetch(w_ff2[:, :, :], w["ff_w2"].rearrange("(j p) n -> p j n", p=128))
            fetch(ident[:, :], w["ident"])
            fetch(pick[:, :], w["pick"])
            with nc.allow_non_contiguous_dma(reason="vectors of a few hundred values, once"):
                fetch(b_ff1[:, :], w["ff_b1"].rearrange("(j p) -> p j", p=128))
                for k in range(3):
                    fetch(gains[:, k, :], w[f"n{k + 1}_g"].rearrange("(c p) -> p c", c=2))
                    fetch(shifts[:, k, :], w[f"n{k + 1}_b"].rearrange("(c p) -> p c", c=2))
            for n, src in (("o1", "o1_b"), ("o2", "o2_b"), ("ff2", "ff_b2"), ("out", "b_out")):
                fetch(biases[n][:, :], w[src].rearrange("(o n) -> o n", o=1).broadcast_to([128, D]))
            assert loads == N_WEIGHT_LOADS

            with sp.Fori(0, PAIRS) as i:
                def at(s, key):
                    return i * total[s.name] + order[s.name, key]

                def taken(step, o=0):
                    m = use_no[step] + o
                    return misc_taken[uses[m]], at(misc_taken[uses[m]], m)

                for name, args, m in steps:
                    if name == "load":
                        s, = args
                        b = i * STREAMS + s
                        sp.dma_start(x_sb[s][:, :, :], x[bass.ds(b, 1)].rearrange("o (t p) d -> p (o t) d", p=128)).then_inc(x_in[s], 16)
                        sp.dma_start(ctx_sb[s][:, :, :], ctx[bass.ds(b, 1)].rearrange("o (t p) d -> p (o t) d", p=128)).then_inc(c_in[s], 16)
                        sp.dma_start(ca_sb[s][:, :], ctx[bass.ds(b, 1), J - CA:J, :].rearrange("o t d -> (o t) d")).then_inc(c_in[s], 16)
                    elif name in SPLIT_STEPS:
                        f = args[0] if name in ("q", "k", "kctx") else CAM
                        s = args[-1]
                        is_q = name in ("q", "camq")
                        last = split_no[m] + len(MISC_USES[name]) - 1
                        scr = (q_scr if is_q else k_scr)[f.name][s]
                        src = (parts_q if is_q else parts_k)[f.name][s]
                        sp.wait_ge(split_done, at(split_done, last))
                        stored = parts_out["q" if is_q else "k", f.name][s]
                        for c in range(2):
                            sp.dma_start(scr[:, c * HALF:(c + 1) * HALF, :].rearrange("p r t -> r p t"),
                                         src[:, :, c, 0:scr.shape[2]]).then_inc(stored, 16)
                    elif name in ("spreadk", "spreadq"):
                        f, s = args
                        if name == "spreadk":
                            if f is SELF:
                                sp.wait_ge(zeros_done, at(zeros_done, ("zeros", s)))
                            elif f is CROSS:
                                sp.wait_ge(*taken(("EVT", last_group["self", s])))
                            else:
                                sp.wait_ge(ones_done, at(ones_done, ("ones", s)))
                            sp.sem_inc(passed, 1)
                        stored = parts_out[name[-1], f.name][s]
                        sp.wait_ge(stored, at(stored, 0))
                        for first, copies, q_part in ROW_LOADS:
                            rows = slice(first * f.dh, (first + copies) * f.dh)
                            if name == "spreadq":
                                sp.dma_start(q_rows[f.name][s][rows, :, 0:f.nq],
                                             q_scr[f.name][s][q_part:q_part + 1].rearrange("p (r h) t -> p r h t", r=f.dh)
                                             .broadcast_to([copies, f.dh, f.heads, f.nq])).then_inc(rows_in[f.name][s], 16)
                            else:
                                cols = k_scr[f.name][s].shape[2]
                                sp.dma_start(k_rows[f.name][s][rows, :, 0:cols],
                                             k_scr[f.name][s][0:copies].rearrange("p (r h) t -> (p r) h t", r=f.dh))\
                                    .then_inc(rows_in[f.name][s], 16)
                    elif name == "MT":
                        n, = args
                        f, s, g = seq[n]
                        sp.wait_ge(*taken(("MT", n)))
                        sp.dma_start(q_rows[f.name][s][f.m_row:f.m_row + 2, GH * g:GH * g + GH, 0:f.nq],
                                     mT[n % 2][:, 0:f.nq]).then_inc(m_in[n % 2], 16)
                    elif name == "fin":
                        s, = args
                        sp.wait_ge(*taken(("fin", s)))
                        sp.sem_inc(passed, 1)
                        sp.dma_start(out[bass.ds(i * STREAMS + s, 1)].rearrange("o (t p) d -> p (o t) d", p=128),
                                     y_sb[s][:, :, :]).then_inc(y_out, 16)
                sp.wait_ge(y_out, at(y_out, ("fin", 1)))
                sp.sem_inc(passed, 1)


        w_q = {"self": wide["q1"], "cross": wide["q2"], "text": wide["Wq"]}
        w_k = {"self": wide["k1"], "cross": thin["k2"], "text": thin["Wk"]}
        w_v = {"self": wide["v1"], "cross": thin["v2"], "text": thin["Wv"]}
        w_o = {"self": wide["o1"], "cross": wide["o2"], "text": wide["Wout"]}

        @block.tensor
        def _(pe):
            pe.wait_ge(w_in, 16 * N_WEIGHT_LOADS)
            pe.wait_ge(ready0, READY0)
            with pe.Fori(0, PAIRS) as i:
                def at(s, key):
                    return i * total[s.name] + order[s.name, key]

                def taken(step, o=0):
                    m = use_no[step] + o
                    return misc_taken[uses[m]], at(misc_taken[uses[m]], m)

                def bank_free(m):
                    if m >= 2:
                        s_read = misc_taken[uses[m - 2]]
                        pe.wait_ge(s_read, at(s_read, m - 2))
                    return misc[m % 2]

                def turn(m, src, q_rows_n):
                    for t in range(len(q_rows_n)):
                        for c in range(2):
                            n_q = q_rows_n[t]
                            last = nc.tensor.transpose(misc[m % 2][0:HALF, c * 256 + t * 128:c * 256 + t * 128 + n_q],
                                                       src[0:n_q, t, c * HALF:(c + 1) * HALF],
                                                       ident[0:n_q, 0:n_q])
                    last.then_inc(misc_full, 1)

                def project_T(m, weight, rhs, n):
                    for o in range(2):
                        for c in range(2):
                            last = nc.tensor.matmul(misc[m % 2][0:HALF, o * 256:o * 256 + n],
                                                    weight[:, c, o * HALF:(o + 1) * HALF], rhs[:, c, 0:n],
                                                    start=(c == 0), stop=(c == 1))
                    last.then_inc(misc_full, 1)

                def project_tok(m, lhs, weight):
                    for t in range(TT):
                        for c in range(2):
                            last = nc.tensor.matmul(misc[m % 2][:, t * D:(t + 1) * D], lhs[:, c, t * 128:(t + 1) * 128],
                                                    weight[:, c, :], start=(c == 0), stop=(c == 1))
                    last.then_inc(misc_full, 1)

                for name, args, m in steps:
                    if name == "ctxT":
                        s, = args
                        bank_free(m)
                        pe.wait_ge(c_in[s], at(c_in[s], 0))
                        for t in range(JT):
                            last = nc.tensor.transpose(misc[m % 2][0:CD, t * 128:(t + 1) * 128], ctx_sb[s][:, t, :], ident[:, :])
                        last.then_inc(misc_full, 1)
                    elif name == "lnT":
                        k, s = args
                        bank_free(m)
                        pe.wait_ge(xn_done, at(xn_done, ("ln", k, s)))
                        turn(m, xn[s], [128] * TT)
                    elif name == "xT":
                        s, = args
                        bank_free(m)
                        pe.wait_ge(x_by_row, at(x_by_row, ("ff2", s)))
                        turn(m, xn[s], [128] * TT)
                    elif name in ("q", "k"):
                        f, s = args
                        bank_free(m)
                        if f is TEXT:
                            pe.wait_ge(xh_done, at(xh_done, ("xT", s)))
                        else:
                            pe.wait_ge(*taken(("lnT", 0 if f is SELF else 1, s)))
                        project_T(m, (w_q if name == "q" else w_k)[f.name], hT[s], N)
                    elif name == "kctx":
                        f, s = args
                        pe.wait_ge(*taken(("ctxT", s)))
                        for o in range(2):
                            bank_free(m + o)
                            nc.tensor.matmul(misc[(m + o) % 2][0:HALF, :], w_k[f.name][:, o * HALF:(o + 1) * HALF], ctxT[s][:, :],
                                             start=True, stop=True).then_inc(misc_full, 1)
                    elif name == "v":
                        f, s = args
                        bank_free(m)
                        pe.wait_ge(*taken(("lnT", 0, s)))
                        project_tok(m, hT[s], w_v["self"])
                    elif name == "vctx":
                        f, s = args
                        for o in range(2):
                            bank_free(m + o)
                            for t in range(2):
                                last = nc.tensor.matmul(misc[(m + o) % 2][:, t * D:(t + 1) * D],
                                                        ctxT[s][:, (2 * o + t) * 128:(2 * o + t + 1) * 128], w_v[f.name][:, :],
                                                        start=True, stop=True)
                            last.then_inc(misc_full, 1)
                    elif name == "camq":
                        s, = args
                        bank_free(m)
                        pe.wait_ge(c_in[s], at(c_in[s], 0))
                        for o in range(2):
                            last = nc.tensor.matmul(misc[m % 2][0:HALF, o * 256:o * 256 + NQA], w_qca[:, o * HALF:(o + 1) * HALF],
                                                    ca_sb[s][:, :], start=True, stop=True)
                        last.then_inc(misc_full, 1)
                    elif name == "cambc":
                        s, = args
                        pe.wait_ge(wide_done, at(wide_done, ("ctxT", s)))
                        for o in range(4):
                            bank_free(m + o)
                            for t in range(2):
                                last = nc.tensor.matmul(misc[(m + o) % 2][0:NQA, t * D:(t + 1) * D],
                                                        ca_wide[s][:, 2 * (o % 2) + t, :], thin["Wk_ca" if o < 2 else "Wv_ca"][:, :],
                                                        start=True, stop=True)
                            last.then_inc(misc_full, 1)
                    elif name == "outT":
                        f, s = args
                        bank_free(m)
                        pe.wait_ge(*taken(("EVT", last_group[f.name, s])))
                        turn(m, o_tok[s], [128] * TT)
                    elif name == "out":
                        f, s = args
                        bank_free(m)
                        pe.wait_ge(*taken(("outT", f.name, s)))
                        project_tok(m, oT[s], w_o[f.name])
                    elif name == "ff1":
                        s, = args
                        pe.wait_ge(*taken(("lnT", 2, s)))
                        for j in range(FF // 128):
                            bank_free(m + j)
                            for o, col in enumerate((j * 128, FF + j * 128)):
                                for c in range(2):
                                    last = nc.tensor.matmul(misc[(m + j) % 2][:, o * 256:(o + 1) * 256], w_ff1[:, c, col:col + 128],
                                                            hT[s][:, c, :], start=(c == 0), stop=(c == 1))
                            last.then_inc(misc_full, 1)
                    elif name == "ff2":
                        s, = args
                        bank_free(m)
                        pe.wait_ge(ff_done, at(ff_done, ("gelu", s)))
                        for t in range(TT):
                            for j in range(FF // 128):
                                last = nc.tensor.matmul(misc[m % 2][:, t * D:(t + 1) * D], ff_a[:, j, t * 128:(t + 1) * 128],
                                                        w_ff2[:, j, :], start=(j == 0), stop=(j == FF // 128 - 1))
                        last.then_inc(misc_full, 1)
                    elif name == "cam2T":
                        s, = args
                        bank_free(m)
                        pe.wait_ge(*taken(("EVT", last_group["cam", s])))
                        turn(m, o_cam[s], [NQA])
                    elif name == "cam2q":
                        s, = args
                        bank_free(m)
                        pe.wait_ge(*taken(("cam2T", s)))
                        for c in range(2):
                            last = nc.tensor.matmul(misc[m % 2][0:NQA, 0:D], oT[s][:, c, 0:NQA], wide["Wq"][:, c, :],
                                                    start=(c == 0), stop=(c == 1))
                        last.then_inc(misc_full, 1)
                    elif name == "hsumT":
                        s, = args
                        bank_free(m)
                        pe.wait_ge(*taken(("EVT", last_group["text", s])))
                        pe.wait_ge(cam_done, at(cam_done, ("cam2", s)))
                        for c in range(2):
                            for t in range(TT):
                                place = misc[m % 2][0:HALF, c * 256 + t * 128:c * 256 + (t + 1) * 128]
                                nc.tensor.matmul(place, cam_out[s][:, c * HALF:(c + 1) * HALF], pick[:, t * 128:(t + 1) * 128],
                                                 start=True, stop=False)
                                last = nc.tensor.matmul(place, o_tok[s][:, t, c * HALF:(c + 1) * HALF], ident[:, :],
                                                        start=False, stop=True)
                        last.then_inc(misc_full, 1)
                    elif name == "fin":
                        s, = args
                        bank_free(m)
                        pe.wait_ge(*taken(("hsumT", s)))
                        project_tok(m, oT[s], w_o["text"])
                    elif name == "MX":
                        n, fill = args
                        f, s, g = seq[n]
                        no = fill_no[args]
                        if g == 0 and fill == 0:
                            pe.wait_ge(rows_in[f.name][s], at(rows_in[f.name][s], 0))
                        if no >= MX_BANKS:
                            pe.wait_ge(mx_read, at(mx_read, no - MX_BANKS))
                        for r in range(f.per_bank):
                            k, t = divmod(fill * f.per_bank + r, len(f.q_tiles))
                            q0, n_q = f.q_tiles[t]
                            last = nc.tensor.matmul(mx_bank[no % MX_BANKS][0:n_q, r * f.nk:(r + 1) * f.nk],
                                                    q_rows[f.name][s][0:f.max_rows, GH * g + k, q0:q0 + n_q],
                                                    k_rows[f.name][s][0:f.max_rows, GH * g + k, 0:f.nk], start=True, stop=True)
                        last.then_inc(mx_full, 1)
                    elif name == "MT":
                        n, = args
                        f, s, g = seq[n]
                        bank_free(m)
                        pe.wait_ge(m_split, at(m_split, n))
                        for t, (q0, n_q) in enumerate(f.q_tiles):
                            last = nc.tensor.transpose(misc[m % 2][:, :].bitcast(BF16)[0:2 * GH, q0:q0 + n_q],
                                                       m_parts[n % 2][0:n_q, t, :, :].rearrange("p a k -> p (a k)"), ident_bf[0:n_q, 0:n_q])
                        last.then_inc(misc_full, 1)
                    elif name == "ST":
                        n, p, u, k = args
                        f, s, g = seq[n]
                        no = GH * u + k
                        if p == 0 and k == 0:
                            pe.wait_ge(m_in[n % 2], at(m_in[n % 2], n))
                        if no >= ST_BANKS:
                            pe.wait_ge(exp_done, at(exp_done, no - ST_BANKS))
                        for half in range(2):
                            kt = 2 * p + half
                            ks = f.k_tiles[kt]
                            last = nc.tensor.matmul(st_bank[no % ST_BANKS][0:ks, half * f.nq:(half + 1) * f.nq],
                                                    k_rows[f.name][s][0:f.st_rows, GH * g + k, kt * 128:kt * 128 + ks],
                                                    q_rows[f.name][s][0:f.st_rows, GH * g + k, 0:f.nq], start=True, stop=True)
                        last.then_inc(st_full, 1)
                    elif name == "PV":
                        n, p, u = args
                        f, s, g = seq[n]
                        pe.wait_ge(exp_done, at(exp_done, GH * u + GH - 1))
                        if g == 0 and p == 0:
                            if f is CAM:
                                pe.wait_ge(cv_done, at(cv_done, ("xT", s)))
                            else:
                                pe.wait_ge(*(taken(("v", "self", s)) if f is SELF else taken(("vctx", f.name, s), 1)))
                        if p == 0 and n:
                            pe.wait_ge(o_read, at(o_read, n - 1))
                        for half in range(2):
                            kt = 2 * p + half
                            ks = f.k_tiles[kt]
                            for k in range(GH):
                                last = nc.tensor.matmul(o_bank[HW * k:HW * (k + 1), 0:f.nq], v_rows[f.name][s][0:ks, kt, GH * g + k, :],
                                                        probs[0:ks, u % P_RING, k, half * f.nq:(half + 1) * f.nq],
                                                        start=(kt == 0), stop=(kt == len(f.k_tiles) - 1))
                        last.then_inc(pv_done, 1)
                    elif name == "EVT":
                        n, = args
                        f, s, g = seq[n]
                        bank_free(m)
                        pe.wait_ge(o_read, at(o_read, n))
                        for t, (q0, n_q) in enumerate(f.q_tiles):
                            last = nc.tensor.transpose(misc[m % 2][0:n_q, t * 128:(t + 1) * 128], o_sb[n % 2][:, q0:q0 + n_q], ident[:, :])
                        last.then_inc(misc_full, 1)
                for e in "AD":
                    m_last = max(m for m, u_ in enumerate(uses) if u_ == e)
                    pe.wait_ge(misc_taken[e], at(misc_taken[e], m_last))
                pe.wait_ge(mx_read, at(mx_read, len(fill_no) - 1))
                pe.wait_ge(exp_done, at(exp_done, GH * n_units - 1))
                pe.wait_ge(o_read, at(o_read, n_groups - 1))

        @block.scalar
        def _(act):
            act.wait_ge(w_in, 16 * N_WEIGHT_LOADS)
            for wt, f in by_row:
                chunks = wt.shape[1] if len(wt.shape) == 3 else 1
                for c in range(chunks):
                    dst = wt[:, c, :] if len(wt.shape) == 3 else wt[:, :]
                    nc.scalar.copy(dst.rearrange("p (r h) -> p r h", h=f.heads),
                                   raw[wt.name][:, c * D:(c + 1) * D].rearrange("p (h r) -> p r h", h=f.heads)).then_inc(ready0, 1)
            act.wait_ge(ready0, READY0)
            with act.Fori(0, PAIRS) as i:
                def at(s, key):
                    return i * total[s.name] + order[s.name, key]

                def taken(step, o=0):
                    m = use_no[step] + o
                    return misc_taken[uses[m]], at(misc_taken[uses[m]], m)

                for name, args, m in steps:
                    if name in ("ctxT", "lnT", "v", "outT", "cam2T", "cam2q", "hsumT", "MT") or name in SPLIT_STEPS and name != "kctx":
                        act.wait_ge(misc_full, at(misc_full, m))
                    if name == "ctxT":
                        s, = args
                        nc.scalar.copy(ctxT[s][:, :], misc[m % 2][0:CD, :]).then_inc(misc_taken["A"], 1)
                    elif name == "lnT":
                        k, s = args
                        for c in range(2):
                            last = nc.scalar.activation(hT[s][:, c, :], misc[m % 2][0:HALF, c * 256:(c + 1) * 256], ACT.Identity,
                                                        bias=shifts[:, k, c:c + 1], scale=gains[:, k, c:c + 1])
                        last.then_inc(misc_taken["A"], 1)
                    elif name in SPLIT_STEPS:
                        s = args[-1]
                        if name == "xT":
                            nc.scalar.copy(hT[s][:, :, :], misc[m % 2][0:HALF, :].rearrange("p (c t) -> p c t", c=2)).then_inc(xh_done, 1)
                        for o in range(len(MISC_USES[name])):
                            if name == "kctx":
                                act.wait_ge(misc_full, at(misc_full, m + o))
                            dst, src = split_views(name, args, m, o)
                            nc.scalar.copy(dst[0], src).then_inc(hi_done, 1)
                    elif name in ("v", "vctx"):
                        f, s = args
                        for o in range(len(MISC_USES[name])):
                            if name == "vctx":
                                act.wait_ge(misc_full, at(misc_full, m + o))
                            nc.scalar.copy(v_rows[f.name][s][:, 2 * o:2 * o + 2, :, 0:f.dh],
                                           misc[(m + o) % 2][:, 0:2 * D].rearrange("p (t h d) -> p t h d", t=2, d=f.dh))\
                                .then_inc(misc_taken["A"], 1)
                    elif name in ("outT", "hsumT"):
                        s = args[-1]
                        nc.scalar.copy(oT[s][:, :, :], misc[m % 2][0:HALF, :].rearrange("p (c t) -> p c t", c=2))\
                            .then_inc(misc_taken["A"], 1)
                    elif name == "cam2T":
                        s, = args
                        nc.scalar.copy(oT[s][:, :, 0:NQA], misc[m % 2][0:HALF, :].rearrange("p (c t) -> p c t", c=2)[:, :, 0:NQA])\
                            .then_inc(misc_taken["A"], 1)
                    elif name == "cam2q":
                        nc.scalar.copy(cam_q[:, :].rearrange("p (h r) -> p r h", h=CAM.heads),
                                       misc[m % 2][0:NQA, 0:D].rearrange("p (r h) -> p r h", h=CAM.heads)).then_inc(misc_taken["A"], 1)
                    elif name == "cambc":
                        s, = args
                        for o in range(4):
                            act.wait_ge(misc_full, at(misc_full, m + o))
                            last = nc.scalar.copy((kb if o < 2 else vb)[:, 2 * (o % 2):2 * (o % 2) + 2, :],
                                                  misc[(m + o) % 2][0:NQA, 0:2 * D].rearrange("p (t d) -> p t d", t=2))
                            last.then_inc(misc_taken["A"], 1)
                    elif name == "ff1":
                        s, = args
                        for j in range(FF // 128):
                            act.wait_ge(misc_full, at(misc_full, m + j))
                            nc.scalar.activation(ff_g[:, j, :], misc[(m + j) % 2][:, 256:512], ACT.Identity,
                                                 bias=b_ff1[:, FF // 128 + j:FF // 128 + j + 1]).then_inc(gate_done, 1)
                    elif name == "gelu":
                        s, = args
                        act.wait_ge(gate_done, at(gate_done, ("ff1", s, FF // 128 - 1)))
                        nc.scalar.activation(ff_g[:, :, :], ff_g[:, :, :], ACT.Gelu).then_inc(gelu_done, 1)
                    elif name == "cam2":
                        s, = args
                        act.wait_ge(cam_arg, at(cam_arg, ("cam2", s)))
                        nc.scalar.activation(cam_e[:, :, :], cam_d[:, :, :], ACT.Exp, scale=CAM.scale).then_inc(cam_exp, 1)
                    elif name == "MT":
                        n, = args
                        f, s, g = seq[n]
                        if n >= 2:
                            act.wait_ge(m_in[n % 2], at(m_in[n % 2], n - 2))
                        nc.scalar.copy(mT[n % 2][:, 0:f.nq], misc[m % 2][:, :].bitcast(BF16)[0:2 * GH, 0:f.nq])\
                            .then_inc(misc_taken["A"], 1)
                    elif name == "ST":
                        n, p, u, k = args
                        f, s, g = seq[n]
                        no = GH * u + k
                        act.wait_ge(st_full, at(st_full, no))
                        if k == 0 and u >= P_RING:
                            act.wait_ge(pv_done, at(pv_done, u - P_RING))
                        bank = st_bank[no % ST_BANKS]
                        short = f.k_tiles[2 * p + 1]
                        if short == 128:
                            last = nc.scalar.activation(probs[:, u % P_RING, k, 0:2 * f.nq], bank[:, 0:2 * f.nq], ACT.Exp, scale=f.scale)
                        else:
                            nc.scalar.activation(probs[:, u % P_RING, k, 0:f.nq], bank[:, 0:f.nq], ACT.Exp, scale=f.scale)
                            last = nc.scalar.activation(probs[0:short, u % P_RING, k, f.nq:2 * f.nq], bank[0:short, f.nq:2 * f.nq],
                                                        ACT.Exp, scale=f.scale)
                        last.then_inc(exp_done, 1)
                act.wait_ge(pv_done, at(pv_done, n_units - 1))
                for par in range(2):
                    act.wait_ge(m_in[par], at(m_in[par], max(range(par, n_groups, 2))))

        @block.vector
        def _(dve):
            dve.wait_ge(w_in, 16 * N_WEIGHT_LOADS)
            nc.vector.tensor_copy(ident_bf[:, :], ident[:, :]).then_inc(ready0, 1)
            for s in range(STREAMS):
                nc.vector.memset(v8[s][:, :, :, :], 1.0).then_inc(ready0, 1)
            with dve.Fori(0, PAIRS) as i:
                def at(s, key):
                    return i * total[s.name] + order[s.name, key]

                def taken(step, o=0):
                    m = use_no[step] + o
                    return misc_taken[uses[m]], at(misc_taken[uses[m]], m)

                links = 0

                def link(ins):
                    nonlocal links
                    links += 1
                    ins.then_inc(dve_step, 1)
                    dve.wait_ge(dve_step, i * total[dve_step.name] + links)
                    dve.sem_inc(passed, 1)

                for name, args, m in steps:
                    if name == "ln":
                        k, s = args
                        if k == 0:
                            dve.wait_ge(x_in[s], at(x_in[s], 0))
                        else:
                            dve.wait_ge(*taken(("out", ("self", "cross")[k - 1], s)))
                        nc.vector.bn_stats(stats[s][:, 0, :], x_sb[s][:, 0, :])
                        link(nc.vector.bn_stats(stats[s][:, 1, :], x_sb[s][:, 1, :]))
                        nc.vector.bn_aggr(mean_var[s][:, 0, :], stats[s][:, 0, :])
                        link(nc.vector.bn_aggr(mean_var[s][:, 1, :], stats[s][:, 1, :]))
                        nc.vector.tensor_scalar(var_eps[s][:, :], mean_var[s][:, :, 1], EPS, None, ALU.add).then_inc(var_done, 1)
                        dve.wait_ge(rstd_done, at(rstd_done, ("ln", k, s)))
                        for t in range(TT):
                            last = nc.vector.tensor_scalar(xn[s][:, t, :], x_sb[s][:, t, :], mean_var[s][:, t, 0:1], rstd[s][:, t:t + 1],
                                                           ALU.subtract, ALU.mult)
                        last.then_inc(xn_done, 1)
                    elif name in SPLIT_STEPS:
                        for o in range(len(MISC_USES[name])):
                            no = split_no[m] + o
                            dve.wait_ge(hi_done, at(hi_done, no))
                            if no >= 2:
                                dve.wait_ge(split_done, at(split_done, no - 2))
                            dst, src = split_views(name, args, m, o)
                            nc.vector.tensor_tensor(rest_view(no, dst[0]), src, dst[0], ALU.subtract)\
                                .then_inc(misc_taken["D"], 1)
                    elif name in ("out", "ff2"):
                        s = args[-1]
                        dve.wait_ge(misc_full, at(misc_full, m))
                        key = ("ln", 2, s) if name == "ff2" else ("ln", 0 if args[0] is SELF else 1, s)
                        dve.wait_ge(xb_done, at(xb_done, key))
                        if name == "ff2":
                            dve.wait_ge(*taken(("lnT", 2, s)))
                            nc.vector.tensor_tensor(xn[s][:, :, :].rearrange("p t (r h) -> p t h r", h=CAM.heads),
                                                    misc[m % 2][:, 0:TT * D].rearrange("p (t h r) -> p t h r", t=TT, h=CAM.heads),
                                                    xb_sb[s][:, :, :].rearrange("p t (h r) -> p t h r", h=CAM.heads), ALU.add)\
                                .then_inc(x_by_row, 1)
                        nc.vector.tensor_tensor(x_sb[s][:, :, :], misc[m % 2][:, 0:TT * D].rearrange("p (t d) -> p t d", t=TT),
                                                xb_sb[s][:, :, :], ALU.add)\
                            .then_inc(misc_taken["D"], 1)
                    elif name == "ff1":
                        s, = args
                        for j in range(FF // 128):
                            dve.wait_ge(gate_done, at(gate_done, ("ff1", s, j)))
                            nc.vector.tensor_scalar(ff_a[:, j, :], misc[(m + j) % 2][:, 0:256], b_ff1[:, j:j + 1], None, ALU.add)\
                                .then_inc(misc_taken["D"], 1)
                    elif name == "gelu":
                        s, = args
                        dve.wait_ge(gelu_done, at(gelu_done, ("gelu", s)))
                        dve.wait_ge(*taken(("ff1", s), FF // 128 - 1))
                        nc.vector.tensor_tensor(ff_a[:, :, :], ff_a[:, :, :], ff_g[:, :, :], ALU.mult).then_inc(ff_done, 1)
                    elif name == "MX":
                        n, fill = args
                        f, s, g = seq[n]
                        no = fill_no[args]
                        if fill == 0 and n >= 2:
                            dve.wait_ge(m_split, at(m_split, n - 2))
                        dve.wait_ge(mx_full, at(mx_full, no))
                        n_q = min(128, f.nq)
                        nc.vector.tensor_reduce(neg_max[n % 2][0:n_q, fill * f.per_bank:(fill + 1) * f.per_bank],
                                                mx_bank[no % MX_BANKS][0:n_q, 0:f.per_bank * f.nk].rearrange("p (r k) -> p r k", k=f.nk),
                                                X, ALU.max, negate=True).then_inc(mx_read, 1)
                    elif name == "NM":
                        n, = args
                        f, s, g = seq[n]
                        nqt = len(f.q_tiles)
                        n_q = min(128, f.nq)
                        view = neg_max[n % 2][0:n_q, 0:GH * nqt].rearrange("p (k t) -> p t k", t=nqt)
                        dve.wait_ge(mx_read, at(mx_read, fill_no[n, f.fills - 1]))
                        if n >= 2:
                            dve.wait_ge(misc_full, at(misc_full, turn_use[n - 2]))
                        link(nc.vector.tensor_copy(m_parts[n % 2][0:n_q, 0:nqt, 0, :], view))
                        nc.vector.tensor_tensor(m_parts[n % 2][0:n_q, 0:nqt, 1, :], view, m_parts[n % 2][0:n_q, 0:nqt, 0, :],
                                                ALU.subtract).then_inc(m_split, 1)
                    elif name == "EVC":
                        n, u = args
                        f, s, g = seq[n]
                        dve.wait_ge(pv_done, at(pv_done, u))
                        nc.vector.tensor_copy(o_sb[n % 2][:, 0:f.nq], o_bank[:, 0:f.nq]).then_inc(o_read, 1)
                    elif name == "EVT":
                        n, = args
                        f, s, g = seq[n]
                        nqt = len(f.q_tiles)
                        n_q = min(128, f.nq)
                        if n >= 2:
                            dve.wait_ge(*taken(("EVT", n - 2)))
                        dve.wait_ge(misc_full, at(misc_full, m))
                        view = misc[m % 2][0:n_q, 0:nqt * 128].rearrange("p (t k c) -> p t k c", t=nqt, k=GH)
                        link(nc.vector.reciprocal(recip[n % 2][0:n_q, 0:nqt, :], view[:, :, :, HW - 1]))
                        if f is CAM:
                            dst = o_cam[s][:, :, :].rearrange("p t (c h) -> p t h c", h=f.heads)[:, :, GH * g:GH * (g + 1), :]
                        else:
                            dst = o_tok[s][0:n_q, 0:nqt, GH * g * f.dh:GH * (g + 1) * f.dh].rearrange("p t (k c) -> p t k c", k=GH)
                        nc.vector.tensor_tensor(dst,
                                                view[:, :, :, 0:f.dh],
                                                recip[n % 2][0:n_q, 0:nqt, :].unsqueeze(3).broadcast_to([n_q, nqt, GH, f.dh]), ALU.mult)\
                            .then_inc(misc_taken["D"], 1)
                    elif name == "cam2":
                        s, = args
                        key = ("cam2", s)
                        dve.wait_ge(cam_prod, at(cam_prod, key))
                        link(nc.vector.tensor_reduce(cam_s[:, :, :], cam_t[:, :, :].rearrange("p j (h d) -> p j h d", h=8), X, ALU.add))
                        link(nc.vector.tensor_reduce(cam_m[:, :], cam_s[:, :, :].rearrange("p j h -> p h j"), X, ALU.max))
                        nc.vector.tensor_tensor(cam_d[:, :, :], cam_s[:, :, :], cam_m[:, :].unsqueeze(1).broadcast_to([NQA, CA, 8]),
                                                ALU.subtract).then_inc(cam_arg, 1)
                        dve.wait_ge(cam_exp, at(cam_exp, key))
                        link(nc.vector.tensor_reduce(cam_z[:, :], cam_e[:, :, :].rearrange("p j h -> p h j"), X, ALU.add))
                        link(nc.vector.reciprocal(cam_z[:, :], cam_z[:, :]))
                        nc.vector.tensor_tensor(cam_e[:, :, :], cam_e[:, :, :], cam_z[:, :].unsqueeze(1).broadcast_to([NQA, CA, 8]),
                                                ALU.mult).then_inc(cam_p, 1)
                        dve.wait_ge(cam_pv, at(cam_pv, key))
                        nc.vector.tensor_reduce(cam_out[s][:, :], cam_t[:, :, :].rearrange("p j x -> p x j"), X, ALU.add).then_inc(cam_done, 1)
                    elif name == "fin":
                        s, = args
                        dve.wait_ge(misc_full, at(misc_full, m))
                        dve.wait_ge(xb_done, at(xb_done, ("xT", s)))
                        nc.vector.tensor_tensor(y_sb[s][:, :, :], misc[m % 2][:, 0:TT * D].rearrange("p (t d) -> p t d", t=TT),
                                                xb_sb[s][:, :, :], ALU.add)\
                            .then_inc(misc_taken["D"], 1)
                assert links == total[dve_step.name], links

        @block.gpsimd
        def _(pool):
            pool.wait_ge(w_in, 16 * N_WEIGHT_LOADS)
            nc.gpsimd.memset(minus_half[:, :], -0.5).then_inc(ready0, 1)
            for s in range(STREAMS):
                nc.gpsimd.memset(q8[s][:, :, :].bitcast(F32), 0.0).then_inc(ready0, 1)
                nc.gpsimd.memset(k8[s][:, :, :].bitcast(F32), 0.0).then_inc(ready0, 1)
            pool.wait_ge(ready0, READY0 - 2)
            for s in range(STREAMS):
                nc.gpsimd.memset(k8[s][SELF.m_row:SELF.m_row + 2, :, :], 1.0).then_inc(ready0, 1)
            pool.wait_ge(ready0, READY0)
            with pool.Fori(0, PAIRS) as i:
                def at(s, key):
                    return i * total[s.name] + order[s.name, key]

                def taken(step, o=0):
                    m = use_no[step] + o
                    return misc_taken[uses[m]], at(misc_taken[uses[m]], m)

                for name, args, m in steps:
                    if name == "ctxT":
                        s, = args
                        pool.wait_ge(*taken(("ctxT", s)))
                        pool.sem_inc(passed, 1)
                        nc.gpsimd.tensor_copy(ca_wide[s][:, :, :], ctxT[s][:, J - CA:J].unsqueeze(2).broadcast_to([CD, CA, NQA]))\
                            .then_inc(wide_done, 1)
                    elif name == "zeros":
                        s, = args
                        nc.gpsimd.memset(q8[s][:, 0:12, :].bitcast(F32), 0.0)
                        nc.gpsimd.memset(k8[s][:, 0:12, :].bitcast(F32), 0.0).then_inc(zero_step, 1)
                        pool.wait_ge(zero_step, i * total[zero_step.name] + order[zeros_done.name, ("zeros", s)])
                        pool.sem_inc(passed, 1)
                        nc.gpsimd.memset(k8[s][SELF.m_row:SELF.m_row + 2, 0:12, :], 1.0).then_inc(zeros_done, 1)
                        pool.wait_ge(zeros_done, at(zeros_done, ("zeros", s)))
                        pool.sem_inc(passed, 1)
                    elif name == "ones":
                        s, = args
                        pool.wait_ge(*taken(("EVT", last_group["cross", s])))
                        pool.sem_inc(passed, 1)
                        nc.gpsimd.memset(k8[s][96:128, 0:12, :], 1.0).then_inc(ones_done, 1)
                        pool.wait_ge(ones_done, at(ones_done, ("ones", s)))
                        pool.sem_inc(passed, 1)
                    elif name == "ln":
                        k, s = args
                        pool.wait_ge(var_done, at(var_done, ("ln", k, s)))
                        nc.gpsimd.tensor_tensor(rstd[s][:, :], var_eps[s][:, :], minus_half[:, :], ALU.pow).then_inc(rstd_done, 1)
                        bias = biases[("o1", "o2", "ff2")[k]]
                        nc.gpsimd.tensor_tensor(xb_sb[s][:, :, :], x_sb[s][:, :, :], bias[:, :].unsqueeze(1).broadcast_to([128, TT, D]),
                                                ALU.add).then_inc(xb_done, 1)
                    if name == "xT":
                        s, = args
                        pool.wait_ge(*taken(("ff2", s)))
                        pool.sem_inc(passed, 1)
                        nc.gpsimd.tensor_copy(vc_[s][:, :, :, 0:CAM.dh], x_sb[s][:, :, :].rearrange("p t (h d) -> p t h d", d=CAM.dh))\
                            .then_inc(cv_done, 1)
                        nc.gpsimd.tensor_tensor(xb_sb[s][:, :, :], x_sb[s][:, :, :], biases["out"][:, :].unsqueeze(1).broadcast_to([128, TT, D]),
                                                ALU.add).then_inc(xb_done, 1)
                    if name in SPLIT_STEPS:
                        for o in range(len(MISC_USES[name])):
                            no = split_no[m] + o
                            pool.wait_ge(misc_taken["D"], at(misc_taken["D"], m + o))
                            dst, src = split_views(name, args, m, o)
                            rest_v = rest_view(no, dst[0])
                            pool.sem_inc(passed, 1)
                            nc.gpsimd.tensor_copy(dst[1], rest_v).then_inc(pool_step, 1)
                            pool.wait_ge(pool_step, i * n_splits + no + 1)
                            nc.gpsimd.tensor_tensor(dst[2], rest_v, dst[1], ALU.subtract).then_inc(split_done, 1)
                    elif name == "cam2":
                        s, = args
                        pool.wait_ge(*taken(("cam2q", s)))
                        nc.gpsimd.tensor_tensor(cam_t[:, :, :], kb[:, :, :], cam_q[:, :].unsqueeze(1).broadcast_to([NQA, CA, D]), ALU.mult)\
                            .then_inc(cam_prod, 1)
                        pool.wait_ge(cam_p, at(cam_p, ("cam2", s)))
                        nc.gpsimd.tensor_tensor(cam_t[:, :, :].rearrange("p j (h d) -> p j h d", h=8),
                                                vb[:, :, :].rearrange("p j (h d) -> p j h d", h=8),
                                                cam_e[:, :, :].unsqueeze(3).broadcast_to([NQA, CA, 8, CAM.dh]), ALU.mult)\
                            .then_inc(cam_pv, 1)


def kernel(**inputs):
    import numpy as _np
    import concourse.bacc as _bacc
    from concourse import mybir as _mybir
    from concourse.bass_utils import run_bass_kernel_spmd as _run

    nc = _bacc.Bacc("TRN2", target_bir_lowering=False, num_devices=1)
    arrays, aps = {}, {}

    def take(name, a):
        a = _np.ascontiguousarray(a)
        arrays[f"in_{name}_dram"] = a
        aps[name] = nc.dram_tensor(f"in_{name}_dram", a.shape, _mybir.dt.from_np(a.dtype), kind="ExternalInput").ap()

    take("x", inputs["x"])
    take("ctx", inputs["ctx_768"])
    for short, name in WEIGHTS.items():
        take(short, inputs[name])
    take("ident", _np.eye(128, dtype=_np.float32))
    rows = _np.linspace(0, NQA - 1, N).astype(_np.int64)
    take("pick", (_np.arange(NQA)[:, None] == rows[None, :]).astype(_np.float32))
    out = nc.dram_tensor("out_0_dram", (B, N, D), F32, kind="ExternalOutput").ap()
    two_blocks(nc, aps["x"], aps["ctx"], aps, out)
    r = _run(nc, [arrays], core_ids=[0])
    return r.results[0]["out_0_dram"]
```

```python
from contextlib import ExitStack

import numpy as np

import concourse.bass as bass
from concourse import mybir

ALU = mybir.AluOpType
ACT = mybir.ActivationFunctionType
F32 = mybir.dt.float32
BF16 = mybir.dt.bfloat16
X = mybir.AxisListType.X

B, N, D = 8, 256, 160
J, CD = 512, 96
FF = 4 * D
CA = 4
NQA = CD
HALF = D // 2
TT = N // 128
JT = J // 128
EPS = 1e-5
STREAMS = 2
READY0 = 4 + 2 + 4
READY1 = 7
PAIRS = B // STREAMS
TWO_ONES = float(np.array([0x3F803F80], np.uint32).view(np.float32)[0])
GH = 4
HW = 32
P_RING = 2
ST_BANKS = 3
MX_BANKS = 2
M_ROW = 120
LEAD = 3


class Family:

    def __init__(self, name, heads, dh, nq, nk, buffer_keys):
        self.name, self.heads, self.dh, self.nq, self.nk = name, heads, dh, nq, nk
        self.buffer_keys = buffer_keys
        self.groups = heads // GH
        self.q_tiles = [(t, min(128, nq - t)) for t in range(0, nq, 128)]
        self.k_tiles = [min(128, nk - t) for t in range(0, nk, 128)]
        self.pairs = len(self.k_tiles) // 2
        self.per_bank = 512 // nk
        self.fills = GH * len(self.q_tiles) // self.per_bank
        self.scale = float(dh) ** -0.5
        self.max_rows = 96 if dh == 8 else M_ROW


SELF = Family("self", 20, 8, N, N, J)
CROSS = Family("cross", 20, 8, N, J, J)
TEXT = Family("text", 8, 20, N, J - CA, J)
CAM = Family("cam", 8, 20, NQA, N, N)
FAMILIES = [SELF, CROSS, TEXT, CAM]
Q_PARTS = (0, 0, 0, 1, 1, 2)
K_PARTS = (0, 1, 2, 0, 1, 0)
ROW_LOADS = ((0, 3, 0), (3, 2, 1), (5, 1, 2))

MISC_USES = {
    "ctxT": "A", "lnT": "A", "q": "D", "k": "D", "kctx": "DD", "v": "A", "vctx": "AA",
    "outT": "A", "out": "D", "ff1": "A", "ff2": "D", "xT": "D", "camq": "D", "cambc": "AAAA",
    "cam2T": "A", "cam2q": "A", "hsumT": "A", "fin": "D", "MT": "A", "EVT": "D",
}


SPLIT_STEPS = ("q", "k", "kctx", "camq", "xT")
DVE_LINKS = {"ln": 2, "NM": 1, "EVT": 1, ("cam2", 1): 2, ("cam2", 3): 2}
DVE_LATER = {"q": 1, "k": 1, "kctx": 1, "camq": 1, "xT": 1, "out": 1, "ff2": 1, "fin": 1}
DVE_OTHER = ("ln", "norm", "glu", "cam2")
N_FIRST_LOADS = 1 + 3 + 6
N_WEIGHT_LOADS = 6 + 6 + 1 + 2 + 1 + 1 + 4
WEIGHTS = {
    "q1": "L0_xattn_q1", "k1": "L0_xattn_k1", "v1": "L0_xattn_v1", "o1": "L0_xattn_o1_w", "o1_b": "L0_xattn_o1_b",
    "q2": "L0_xattn_q2", "k2": "L0_xattn_k2", "v2": "L0_xattn_v2", "o2": "L0_xattn_o2_w", "o2_b": "L0_xattn_o2_b",
    "n1_g": "L0_xattn_n1_g", "n1_b": "L0_xattn_n1_b", "n2_g": "L0_xattn_n2_g", "n2_b": "L0_xattn_n2_b",
    "n3_g": "L0_xattn_n3_g", "n3_b": "L0_xattn_n3_b",
    "ff_w1": "L0_xattn_ff_w1", "ff_b1": "L0_xattn_ff_b1", "ff_w2": "L0_xattn_ff_w2", "ff_b2": "L0_xattn_ff_b2",
    "Wq": "L1_xattn_Wq", "Wk": "L1_xattn_Wk", "Wv": "L1_xattn_Wv", "Wq_ca": "L1_xattn_Wq_ca",
    "Wk_ca": "L1_xattn_Wk_ca", "Wv_ca": "L1_xattn_Wv_ca", "Wout": "L1_xattn_Wout", "b_out": "L1_xattn_b_out",
}


def make_schedules():
    seq = [(f, s, g) for f, s in ((SELF, 0), (SELF, 1), (CROSS, 0), (CROSS, 1)) for g in range(f.groups)]
    seq += [(f, s, g) for s in range(2) for f in (CAM, TEXT) for g in range(f.groups)]
    units = [(n, p) for n, (f, s, g) in enumerate(seq) for p in range(f.pairs)]
    n_groups, n_units = len(seq), len(units)
    first_unit = [units.index((n, 0)) for n in range(n_groups)]
    over = {}
    for u, (n, p) in enumerate(units):
        over[seq[n][0].name, seq[n][1]] = u + 1

    placed = {}

    def chain(unit, delta, *pieces):
        for slot, *step in pieces:
            placed.setdefault(GH * unit + slot, []).append((tuple(step), delta))

    for s in range(2):
        chain(0, 0, (0, "loadc", s), (2, "bias", 0, s))
        c = over["self", s]
        if s == 0:
            chain(c - 3, 0, (0, "ctxT", 0), (2, "kctx", CROSS, 0))
        chain(c, 0, (3, "spreadk", CROSS, s), (5, "outT", SELF, s), (6, "out", SELF, s), (6, "ln", 1, s),
              (7, "norm", 1, s), (7, "bias", 1, s), (9, "lnT", 1, s), (10, "q", CROSS, s), (10, "spreadq", CROSS, s), (10, "vctx", CROSS, s))
        if s == 0:
            chain(c, 0, (10, "ctxT", 1), (10, "kctx", CROSS, 1), (10, "kctx", TEXT, 0), (10, "camq", 0))
        c = over["cross", s]
        if s == 1:
            chain(c - 4, 0, (0, "kctx", TEXT, 1), (4, "camq", 1))
        chain(c, 0, (5, "outT", CROSS, s), (6, "out", CROSS, s), (6, "ln", 2, s),
              (7, "norm", 2, s), (7, "bias", 2, s), (8, "vctx", TEXT, s), (9, "lnT", 2, s), *[(10 + j, "ff1", s, j) for j in range(FF // 128)],
              (15, "gelu", s), (16, "spreadk", TEXT, s), (16, "spreadq", CAM, s), (18, "glu", s),
              (20, "ff2", s), (21, "xT", s), (21, "spreadk", CAM, s), (21, "q", TEXT, s), (21, "spreadq", TEXT, s), (21, "xcopy", s))
        c = over["cam", s]
        chain(c, 0, (4, "cam2T", s), (5, "cam2q", s))
        chain(over["cross", 1] if s == 0 else c - 1, 0, (21 if s == 0 else 8, "cambc", s), *[((22 if s == 0 else 9) + 2 * j, "cam2", s, j) for j in range(6)])
    c = over["cross", 1]
    chain(c, 1, (14, "load", 0), (18, "ln", 0, 0), (19, "norm", 0, 0), (21, "lnT", 0, 0), (21, "k", SELF, 0), (23, "q", SELF, 0),
          (23, "load", 1), (26, "ln", 0, 1), (27, "norm", 0, 1), (28, "lnT", 0, 1), (29, "k", SELF, 1), (30, "q", SELF, 1))
    c = over["text", 0]
    chain(c, 1, (3, "zeros", 0), (6, "spreadk", SELF, 0), (6, "spreadq", SELF, 0), (8, "v", SELF, 0))
    chain(c, 0, (11, "hsumT", 0), (13, "fin", 0))

    split, now = {}, [0]
    body, copied, filled, turned, finished = [], [], {n: seq[n][0].fills for n in range(LEAD)}, {0, 1}, []

    def group(n):
        return n % n_groups, n // n_groups

    def fill_up(n, upto):
        g, delta = group(n)
        while filled.get(n, 0) < upto:
            filled[n] = filled.get(n, 0) + 1
            body.append(("MX", (g, filled[n] - 1), delta))
            if filled[n] == seq[g][0].fills:
                split[n] = now[0]
                body.append(("NM", (g,), delta))

    def turn(n):
        if n not in turned:
            turned.add(n)
            fill_up(n, seq[n % n_groups][0].fills)
            body.append(("MT", (n % n_groups,), n // n_groups))
            copied.append(("MD", (n % n_groups,), n // n_groups))

    def unit_of(n):
        return first_unit[n % n_groups] + n // n_groups * n_units

    split[2] = -1

    def work_ahead(slot):
        quota = 2
        for n in range(n_groups + LEAD):
            f, s, g = seq[n % n_groups]
            width = GH * f.pairs
            if filled.get(n, 0) < f.fills:
                due = (slot - (GH * unit_of(n) - 7 - width) + 1) * f.fills // width
                if due <= 0 or not quota or not {(name, f.name, s, n // n_groups) for name in ("spreadk", "spreadq")} <= set(spread):
                    break
                take_ = min(due, f.fills, filled.get(n, 0) + quota)
                quota -= take_ - filled.get(n, 0)
                fill_up(n, take_)
                if filled[n] < f.fills:
                    break
        for n in range(n_groups + 2):
            if n not in turned and slot >= GH * unit_of(n) - 6:
                if split.get(n, slot) < slot:
                    turn(n)
                break

    spread = [(name, "self", s, 0) for s in range(2) for name in ("spreadk", "spreadq")]
    for u, (n, p) in enumerate(units):
        for k in range(GH):
            slot = now[0] = GH * u + k
            if k == 0 and p == 0:
                turn(n)
                while copied:
                    body.append(copied.pop(0))
            body.append(("ST", (n, p, u, k), 0))
            while copied:
                body.append(copied.pop(0))
            work_ahead(slot)
            if k == 1 and u:
                body.append(("PV", (*units[u - 1], u - 1), 0))
                if p == 0:
                    body.append(("EVC", (n - 1, u - 1), 0))
                    finished.append(n - 1)
            if k == 3 and finished:
                body.append(("EVT", (finished.pop(),), 0))
            for (name, *args), delta in placed.pop(slot, []):
                body.append((name, tuple(args), delta))
                if name in ("spreadk", "spreadq"):
                    spread.append((name, args[0].name, args[1], delta))
    body += [("PV", (*units[-1], n_units - 1), 0), ("EVC", (n_groups - 1, n_units - 1), 0), ("EVT", (n_groups - 1,), 0)]
    for slot in sorted(placed):
        body += [(name, tuple(args), delta) for (name, *args), delta in placed[slot]]
    body += [("zeros", (1,), 1), ("hsumT", (1,), 0), ("spreadk", (SELF, 1), 1), ("v", (SELF, 1), 1), ("spreadq", (SELF, 1), 1), ("fin", (1,), 0)]
    for n in range(LEAD):
        fill_up(n_groups + n, seq[n][0].fills)
    for n in range(2):
        turn(n_groups + n)
    body += copied

    before = [("load", (s,), 1) for s in range(2)]
    before += [(name, (0, s), 1) for s in range(2) for name in ("ln", "norm")]
    for s in range(2):
        before += [("lnT", (0, s), 1), ("k", (SELF, s), 1), ("q", (SELF, s), 1), ("v", (SELF, s), 1),
                   ("spreadk", (SELF, s), 1), ("spreadq", (SELF, s), 1)]
    before += [st for st in body if st[2] == 1 and st[0] in ("MX", "NM", "MT", "MD")]
    assert len(before) == sum(d for _, _, d in body) - 2
    return seq, units, before, body, [st for st in body if st[2] == 0]


class Segment:

    def __init__(self, steps, first, rounds, seq):
        self.starts = {n for n, (f, s, g) in enumerate(seq) if g == 0}
        self.first, self.rounds = first, rounds
        self.steps, self.uses = [], []
        self.use_no, self.split_no, splits = {}, {}, 0
        for name, args, delta in steps:
            m = len(self.uses)
            self.steps.append((name, args, m, delta))
            self.uses.extend(MISC_USES.get(name, ""))
            if name in MISC_USES:
                self.use_no[step_key(name, args)] = m
            if name in SPLIT_STEPS:
                self.split_no[m] = splits
                splits += len(MISC_USES[name])
        self.n_splits = splits
        self.dve_steps = self.later_for_dve()
        assert len(self.uses) % 2 == 0 and splits % 2 == 0
        self.total, self.order, self.start = {}, {}, {}

    def later_for_dve(self):
        steps, held = [], []
        for step in self.steps:
            name, args, m, delta = step
            if name == "ST":
                held = [(st, slots - 1) for st, slots in held]
            banks = len(MISC_USES.get(name, ""))
            while held and (held[0][1] <= 0 or name in DVE_OTHER or name == "MX" and args[0] in self.starts and args[1] == 0 or banks and m + banks - 1 >= held[0][0][2] + 2):
                steps.append(held.pop(0)[0])
            if name in DVE_LATER:
                held.append((step, DVE_LATER[name]))
            else:
                steps.append(step)
        return steps + [st for st, _ in held]

    def of(self, *names):
        return [step_key(name, args) for name, args, _, _ in self.steps if name in names]


def step_key(name, args):
    return (name,) + tuple(a.name if isinstance(a, Family) else a for a in args)


def two_blocks(nc, x, ctx, w, out):
    seq, units, before, body, last_round = make_schedules()
    n_groups, n_units = len(seq), len(units)
    segments = [Segment(before, -1, 1, seq), Segment(body, 0, PAIRS - 1, seq), Segment(last_round, PAIRS - 1, 1, seq)]
    BEFORE, BODY, LAST = segments
    fill_no = {(n, fill): no for no, (n, fill) in
               enumerate((n, fill) for n in range(n_groups) for fill in range(seq[n][0].fills))}

    with ExitStack() as stack:
        def sb(name, shape, dt=F32):
            return stack.enter_context(nc.sbuf_tensor(name, shape, dt))

        def per_stream(name, shape, dt=F32):
            return [sb(f"{name}_{s}", shape, dt) for s in range(STREAMS)]

        def sem(name):
            return stack.enter_context(nc.semaphore(name))

        mx_bank = [stack.enter_context(nc.psum_tensor(f"mx_bank{i}", [128, 512], F32)) for i in range(MX_BANKS)]
        st_bank = [stack.enter_context(nc.psum_tensor(f"st_bank{i}", [128, 512], F32)) for i in range(ST_BANKS)]
        o_bank = stack.enter_context(nc.psum_tensor("o_bank", [128, 512], F32))
        misc = [stack.enter_context(nc.psum_tensor(f"misc{i}", [128, 512], F32)) for i in range(2)]

        wide = {n: sb("w_" + n, [HALF, 2, D]) for n in ("q1", "k1", "v1", "o1", "q2", "o2", "Wq", "Wout")}
        thin = {n: sb("w_" + n, [CD, D]) for n in ("k2", "v2", "Wk", "Wv", "Wk_ca", "Wv_ca")}
        w_qca = sb("w_qca", [CA, D])
        w_ff1 = sb("w_ff1", [HALF, 2, 2 * FF])
        w_ff2 = sb("w_ff2", [128, FF // 128, D])
        b_ff1 = sb("b_ff1", [128, 2 * FF // 128])
        gains = sb("gains", [HALF, 3, 2])
        shifts = sb("shifts", [HALF, 3, 2])
        biases = {n: sb("b_" + n, [128, D]) for n in ("o1", "o2", "ff2", "out")}
        by_row = [(wide["q1"], SELF), (wide["k1"], SELF), (wide["q2"], CROSS), (wide["Wq"], TEXT),
                  (thin["k2"], CROSS), (thin["Wk"], TEXT), (w_qca, CAM)]
        ident = sb("ident", [128, 128])
        ident_bf = sb("ident_bf", [128, 128], BF16)
        pick = sb("pick", [NQA, N])
        minus_half = sb("minus_half", [128, TT])

        x_sb = per_stream("x_sb", [128, TT, D])
        xb_sb = per_stream("xb_sb", [128, TT, D])
        ca_sb = per_stream("ca_sb", [CA, CD])
        ctxT = per_stream("ctxT", [CD, J])
        xn = per_stream("xn", [128, TT, D])
        hT = per_stream("hT", [HALF, 2, N])
        stats = per_stream("stats", [128, TT, 6])
        mean_var = per_stream("mean_var", [128, TT, 2])
        var_eps = per_stream("var_eps", [128, TT])
        rstd = per_stream("rstd", [128, TT])
        q8, k8 = per_stream("q8", [128, 20, N], BF16), per_stream("k8", [128, 20, J], BF16)
        v8 = per_stream("v8", [128, JT, 20, HW])
        qt_ = [a[:, 0:8, :] for a in q8]
        kt_ = [a[:, 0:8, :] for a in k8]
        qc_ = [a[:, 8:11, :].rearrange("p a b -> p (a b)").rearrange("p (h t) -> p h t", h=8) for a in q8]
        kc_ = [a[:, 8:12, :].rearrange("p a b -> p (a b)").rearrange("p (h t) -> p h t", h=8) for a in k8]
        vt_ = [a[:, :, 0:8, :] for a in v8]
        vc_ = [a[:, 0:TT, 8:16, :] for a in v8]
        q_rows = {"self": q8, "cross": q8, "text": qt_, "cam": qc_}
        k_rows = {"self": k8, "cross": k8, "text": kt_, "cam": kc_}
        v_rows = {"self": v8, "cross": v8, "text": vt_, "cam": vc_}
        o_tok = per_stream("o_tok", [128, TT, D])
        o_cam = [sb("o_cam", [NQA, 1, D])] * STREAMS
        turned = per_stream("turned", [128, 2 * N])
        oT = [a[0:HALF, :].rearrange("p (c t) -> p c t", c=2) for a in turned]
        ctx_sb = [a[:, 0:JT * CD].rearrange("p (t d) -> p t d", t=JT) for a in turned]
        q_parts = per_stream("q_parts", [HALF, 3, 2, N], BF16)
        k_parts = per_stream("k_parts", [HALF, 3, 2, J], BF16)
        cq_parts = per_stream("cq_parts", [HALF, 3, 2, NQA], BF16)
        ck_parts = per_stream("ck_parts", [HALF, 3, 2, N], BF16)
        ca_wide = per_stream("ca_wide", [CD, CA, NQA])
        cam_out = [sb("cam_out", [NQA, D])] * STREAMS

        rest = [sb(f"rest{i}", [HALF, 512]) for i in range(2)]
        probs = sb("probs", [128, P_RING, GH, 512])
        neg_max = [sb(f"neg_max{i}", [128, GH * TT]) for i in range(2)]
        m_parts = [sb(f"m_parts{i}", [128, TT, 2, GH], BF16) for i in range(2)]
        mT = [sb(f"mT{i}", [2 * GH, N], BF16) for i in range(2)]
        o_sb = [sb(f"o_sb{i}", [128, N]) for i in range(2)]
        recip = [sb(f"recip{i}", [128, TT, GH]) for i in range(2)]
        ff_a = sb("ff_a", [128, FF // 128, N])
        ff_g = sb("ff_g", [128, FF // 128, N])
        kb = sb("kb", [NQA, CA, D])
        vb = sb("vb", [NQA, CA, D])
        cam_q = sb("cam_q", [NQA, D])
        cam_t = sb("cam_t", [NQA, CA, D])
        cam_s = sb("cam_s", [NQA, CA, 8])
        cam_m = sb("cam_m", [NQA, 8])
        cam_d = sb("cam_d", [NQA, CA, 8])
        cam_e = sb("cam_e", [NQA, CA, 8])
        cam_z = sb("cam_z", [NQA, 8])

        raw, place = {}, 0
        for wt, f in by_row:
            shape = list(wt.shape)
            size = shape[1] * shape[2] if len(shape) == 3 else shape[1]
            raw[wt.name] = probs[0:shape[0], :, :, :].rearrange("p a b c -> p (a b c)")[:, place:place + size]
            place += size

        def scratch(name, cols):
            return [nc.dram_tensor(f"{name}_{s}", [3, D, cols], BF16, kind="Internal").ap() for s in range(STREAMS)]

        q_scr = {f.name: scratch("qs_" + f.name, f.nq) for f in FAMILIES}
        k_scr = {f.name: scratch("ks_" + f.name, N if f in (SELF, CAM) else J) for f in FAMILIES}
        parts_q = {"self": q_parts, "cross": q_parts, "text": q_parts, "cam": cq_parts}
        parts_k = {"self": k_parts, "cross": k_parts, "text": k_parts, "cam": ck_parts}

        w_first = sem("w_first")
        w_in = sem("w_in")
        ready0 = sem("ready0")
        filled1 = sem("filled1")
        ready1 = sem("ready1")
        x_in = [sem(f"x_in{s}") for s in range(2)]
        c_in = [sem(f"c_in{s}") for s in range(2)]
        misc_full = sem("misc_full")
        misc_taken = {"A": sem("misc_taken_act"), "D": sem("misc_taken_dve")}
        mx_full, mx_read = sem("mx_full"), sem("mx_read")
        m_split = sem("m_split")
        m_in = [sem(f"m_in{i}") for i in range(2)]
        st_full, exp_done = sem("st_full"), sem("exp_done")
        pv_done, o_read = sem("pv_done"), sem("o_read")
        hi_done = sem("hi_done")
        mid_done = sem("mid_done")
        split_done = sem("split_done")
        parts_out = {(a, f.name): [sem(f"{a}_out_{f.name}{s}") for s in range(2)] for a in "qk" for f in FAMILIES}
        rows_in = {f.name: [sem(f"rows_in_{f.name}{s}") for s in range(2)] for f in FAMILIES}
        var_done, rstd_done, xn_done = sem("var_done"), sem("rstd_done"), sem("xn_done")
        xh_done, xb_done, x_by_row = sem("xh_done"), sem("xb_done"), sem("x_by_row")
        zeros_done = sem("zeros_done")
        wide_done, cv_done = sem("wide_done"), sem("cv_done")
        gate_done, gelu_done, ff_done = sem("gate_done"), sem("gelu_done"), sem("ff_done")
        cam_prod, cam_arg, cam_exp, cam_p = (sem(n) for n in ("cam_prod", "cam_arg", "cam_exp", "cam_p"))
        cam_pv, cam_done = sem("cam_pv"), sem("cam_done")
        dve_step = sem("dve_step")
        passed = sem("passed")
        y_out = [sem(f"y_out{s}") for s in range(2)]

        per_pair, place_in_pair = {}, {}

        def count_pairs(s, keys, by=1):
            per_pair[s.name] = by * len(keys)
            for i, k in enumerate(keys):
                place_in_pair[s.name, k] = by * (i + 1)

        for s in (mx_full, mx_read):
            count_pairs(s, list(range(len(fill_no))))
        for s in (o_read, m_split):
            count_pairs(s, list(range(n_groups)))
        for par in range(2):
            count_pairs(m_in[par], list(range(par, n_groups, 2)), 16)
        for s in (st_full, exp_done):
            count_pairs(s, list(range(GH * n_units)))
        count_pairs(pv_done, list(range(n_units)))
        for s in range(2):
            count_pairs(x_in[s], [0], 16)
            count_pairs(c_in[s], [0], 32)
            count_pairs(y_out[s], [0], 16)
            for f in FAMILIES:
                count_pairs(rows_in[f.name][s], [0], 16 * 2 * len(ROW_LOADS))
                for a in "qk":
                    count_pairs(parts_out[a, f.name][s], [0], 16 * 2)

        def of_pair(s, pair, key=0):
            return pair * per_pair[s.name] + place_in_pair[s.name, key]

        def count(s, keys_of, by=1):
            start = 0
            for seg in segments:
                keys = keys_of(seg)
                seg.total[s.name], seg.start[s.name] = by * len(keys), start
                for i, k in enumerate(keys):
                    seg.order[s.name, k] = by * (i + 1)
                start += by * len(keys) * seg.rounds

        def in_round(seg, i, s, key):
            at_start = seg.start[s.name]
            return (at_start + (i - seg.first) * seg.total[s.name] if seg is BODY else at_start) + seg.order[s.name, key]

        count(misc_full, lambda seg: list(range(len(seg.uses))))
        for e in "AD":
            count(misc_taken[e], lambda seg, e=e: [m for m, u in enumerate(seg.uses) if u == e])
        for s in (hi_done, mid_done, split_done):
            count(s, lambda seg: list(range(seg.n_splits)))
        for s in (var_done, rstd_done):
            count(s, lambda seg: seg.of("ln"))
        count(xn_done, lambda seg: seg.of("norm"))
        count(xh_done, lambda seg: seg.of("xT"))
        count(x_by_row, lambda seg: seg.of("ff2"))
        count(xb_done, lambda seg: seg.of("bias", "xcopy"))
        count(wide_done, lambda seg: seg.of("ctxT"))
        count(zeros_done, lambda seg: seg.of("zeros"))
        count(cv_done, lambda seg: seg.of("xcopy"))
        count(gate_done, lambda seg: seg.of("ff1"))
        count(gelu_done, lambda seg: seg.of("gelu"))
        count(ff_done, lambda seg: seg.of("glu"))
        for phase, s in enumerate((cam_prod, cam_arg, cam_exp, cam_p, cam_pv, cam_done)):
            count(s, lambda seg, phase=phase: [k for k in seg.of("cam2") if k[2] == phase])
        count(dve_step, lambda seg: [j for j in range(sum(DVE_LINKS.get(name if name != "cam2" else (name, args[1]), 0)
                                                          for name, args, _, _ in seg.steps))])

        last_group = {}
        for n, (f, s, g) in enumerate(seq):
            last_group[f.name, s] = n

        def split_views(name, args, m, o):
            s = args[-1]
            bank = misc[(m + o) % 2][0:HALF, :]
            if name == "kctx":
                return [k_parts[s][:, p, o, :] for p in range(3)], bank
            bank = bank.rearrange("p (c t) -> p c t", c=2)
            if name == "camq":
                return [cq_parts[s][:, p, :, :] for p in range(3)], bank[:, :, 0:NQA]
            if name == "xT":
                return [ck_parts[s][:, p, :, :] for p in range(3)], bank
            if name == "q":
                return [q_parts[s][:, p, :, :] for p in range(3)], bank
            return [k_parts[s][:, p, :, 0:N] for p in range(3)], bank

        def rest_view(no, like):
            shape = list(like.shape)
            if len(shape) == 2:
                return rest[no % 2][:, :]
            return rest[no % 2][:, :].rearrange("p (c t) -> p c t", c=2)[:, :, 0:shape[2]]

        block = stack.enter_context(nc.Block())

        @block.sync
        def _(sp):
            loads, to_signal = 0, w_first

            def fetch(dst, src):
                nonlocal loads
                sp.dma_start(dst, src).then_inc(to_signal, 16)
                loads += 1

            def as_loaded(wt):
                if wt.name not in raw:
                    return wt
                return raw[wt.name].rearrange("p (c n) -> p c n", n=D) if len(wt.shape) == 3 else raw[wt.name]

            for s in range(STREAMS):
                sp.dma_start(x_sb[s][:, :, :], x[s:s + 1].rearrange("o (t p) d -> p (o t) d", p=128)).then_inc(x_in[s], 16)
            fetch(ident[:, :], w["ident"])
            for n in ("k1", "q1", "v1"):
                fetch(as_loaded(wide[n])[:, :, :], w[n].rearrange("(c p) n -> p c n", c=2))
            with nc.allow_non_contiguous_dma(reason="vectors of a few hundred values, once"):
                for k in range(3):
                    fetch(gains[:, k, :], w[f"n{k + 1}_g"].rearrange("(c p) -> p c", c=2))
                    fetch(shifts[:, k, :], w[f"n{k + 1}_b"].rearrange("(c p) -> p c", c=2))
            assert loads == N_FIRST_LOADS
            to_signal = w_in
            for n in wide:
                if n == "Wq":
                    for c in range(2):
                        fetch(as_loaded(wide[n])[:, c, :], w[n].rearrange("(h r) n -> r h n", h=CAM.heads)[c * CAM.dh // 2:(c + 1) * CAM.dh // 2, :, :])
                elif n not in ("k1", "q1", "v1"):
                    fetch(as_loaded(wide[n])[:, :, :], w[n].rearrange("(c p) n -> p c n", c=2))
            for n in thin:
                fetch(as_loaded(thin[n])[:, :], w[n])
            fetch(as_loaded(w_qca)[:, :], w["Wq_ca"])
            fetch(w_ff1[:, :, :], w["ff_w1"].rearrange("(c p) n -> p c n", c=2))
            fetch(w_ff2[:, :, :], w["ff_w2"].rearrange("(j p) n -> p j n", p=128))
            fetch(pick[:, :], w["pick"])
            with nc.allow_non_contiguous_dma(reason="a vector of a few hundred values, once"):
                fetch(b_ff1[:, :], w["ff_b1"].rearrange("(j p) -> p j", p=128))
            for n, src in (("o1", "o1_b"), ("o2", "o2_b"), ("ff2", "ff_b2"), ("out", "b_out")):
                fetch(biases[n][:, :], w[src].rearrange("(o n) -> o n", o=1).broadcast_to([128, D]))
            assert loads == N_FIRST_LOADS + N_WEIGHT_LOADS
            for s in range(STREAMS):
                sp.sem_inc(y_out[s], 16)

            def run_round(seg, i):
                def at(s, key):
                    return in_round(seg, i, s, key)

                def taken(step, o=0):
                    m = seg.use_no[step] + o
                    return misc_taken[seg.uses[m]], at(misc_taken[seg.uses[m]], m)

                for name, args, m, delta in seg.steps:
                    pair = i + delta
                    if name == "load" and seg is not BEFORE:
                        s, = args
                        sp.wait_ge(xb_done, at(xb_done, ("xcopy", s)))
                        sp.sem_inc(passed, 1)
                        sp.dma_start(x_sb[s][:, :, :], x[bass.ds(pair * STREAMS + s, 1)].rearrange("o (t p) d -> p (o t) d", p=128))\
                            .then_inc(x_in[s], 16)
                    elif name == "loadc":
                        s, = args
                        b = pair * STREAMS + s
                        sp.dma_start(ctx_sb[s][:, :, :], ctx[bass.ds(b, 1)].rearrange("o (t p) d -> p (o t) d", p=128)).then_inc(c_in[s], 16)
                        sp.dma_start(ca_sb[s][:, :], ctx[bass.ds(b, 1), J - CA:J, :].rearrange("o t d -> (o t) d")).then_inc(c_in[s], 16)
                    elif name in SPLIT_STEPS:
                        f = args[0] if name in ("q", "k", "kctx") else CAM
                        s = args[-1]
                        is_q = name in ("q", "camq")
                        last = seg.split_no[m] + len(MISC_USES[name]) - 1
                        scr = (q_scr if is_q else k_scr)[f.name][s]
                        src = (parts_q if is_q else parts_k)[f.name][s]
                        sp.wait_ge(split_done, at(split_done, last))
                        stored = parts_out["q" if is_q else "k", f.name][s]
                        for c in range(2):
                            sp.dma_start(scr[:, c * HALF:(c + 1) * HALF, :].rearrange("p r t -> r p t"),
                                         src[:, :, c, 0:scr.shape[2]]).then_inc(stored, 16)
                    elif name in ("spreadk", "spreadq"):
                        f, s = args
                        if name == "spreadk":
                            if seg is BEFORE:
                                sp.wait_ge(ready0, READY0)
                                if s == 1:
                                    sp.wait_ge(filled1, 2)
                            elif f is SELF:
                                sp.wait_ge(zeros_done, at(zeros_done, ("zeros", s)))
                            elif f is CROSS:
                                sp.wait_ge(*taken(("EVT", last_group["self", s])))
                            else:
                                sp.wait_ge(*taken(("EVT", last_group["cross", s])))
                            sp.sem_inc(passed, 1)
                        stored = parts_out[name[-1], f.name][s]
                        sp.wait_ge(stored, of_pair(stored, pair))
                        for first, copies, q_part in ROW_LOADS:
                            rows = slice(first * f.dh, (first + copies) * f.dh)
                            if name == "spreadq":
                                sp.dma_start(q_rows[f.name][s][rows, :, 0:f.nq],
                                             q_scr[f.name][s][q_part:q_part + 1].rearrange("p (r h) t -> p r h t", r=f.dh)
                                             .broadcast_to([copies, f.dh, f.heads, f.nq])).then_inc(rows_in[f.name][s], 16)
                            else:
                                cols = k_scr[f.name][s].shape[2]
                                sp.dma_start(k_rows[f.name][s][rows, :, 0:cols],
                                             k_scr[f.name][s][0:copies].rearrange("p (r h) t -> (p r) h t", r=f.dh))\
                                    .then_inc(rows_in[f.name][s], 16)
                    elif name == "fin":
                        s, = args
                        sp.wait_ge(*taken(("fin", s)))
                        sp.sem_inc(passed, 1)
                        sp.dma_start(out[bass.ds(pair * STREAMS + s, 1)].rearrange("o (t p) d -> p (o t) d", p=128),
                                     xb_sb[s][:, :, :]).then_inc(y_out[s], 16)

            run_round(BEFORE, -1)
            with sp.Fori(0, PAIRS - 1) as i:
                run_round(BODY, i)
            run_round(LAST, PAIRS - 1)
            for s in range(STREAMS):
                sp.wait_ge(y_out[s], 16 * (1 + PAIRS))

        w_q = {"self": wide["q1"], "cross": wide["q2"], "text": wide["Wq"]}
        w_k = {"self": wide["k1"], "cross": thin["k2"], "text": thin["Wk"]}
        w_v = {"self": wide["v1"], "cross": thin["v2"], "text": thin["Wv"]}
        w_o = {"self": wide["o1"], "cross": wide["o2"], "text": wide["Wout"]}

        @block.tensor
        def _(pe):
            pe.wait_ge(w_first, 16 * N_FIRST_LOADS)
            pe.wait_ge(ready0, READY0)
            def run_round(seg, i):
                def at(s, key):
                    return in_round(seg, i, s, key)

                def taken(step, o=0):
                    m = seg.use_no[step] + o
                    return misc_taken[seg.uses[m]], at(misc_taken[seg.uses[m]], m)

                def bank_free(m):
                    if m >= 2:
                        s_read = misc_taken[seg.uses[m - 2]]
                        pe.wait_ge(s_read, at(s_read, m - 2))
                    return misc[m % 2]

                def turn(m, src, q_rows_n):
                    for t in range(len(q_rows_n)):
                        for c in range(2):
                            n_q = q_rows_n[t]
                            last = nc.tensor.transpose(misc[m % 2][0:HALF, c * 256 + t * 128:c * 256 + t * 128 + n_q],
                                                       src[0:n_q, t, c * HALF:(c + 1) * HALF],
                                                       ident[0:n_q, 0:n_q])
                    last.then_inc(misc_full, 1)

                def project_T(m, weight, rhs, n):
                    for o in range(2):
                        for c in range(2):
                            last = nc.tensor.matmul(misc[m % 2][0:HALF, o * 256:o * 256 + n],
                                                    weight[:, c, o * HALF:(o + 1) * HALF], rhs[:, c, 0:n],
                                                    start=(c == 0), stop=(c == 1))
                    last.then_inc(misc_full, 1)

                def project_tok(m, lhs, weight):
                    for t in range(TT):
                        for c in range(2):
                            last = nc.tensor.matmul(misc[m % 2][:, t * D:(t + 1) * D], lhs[:, c, t * 128:(t + 1) * 128],
                                                    weight[:, c, :], start=(c == 0), stop=(c == 1))
                    last.then_inc(misc_full, 1)

                for name, args, m, delta in seg.steps:
                    pair = i + delta
                    if name == "ctxT":
                        s, = args
                        bank_free(m)
                        pe.wait_ge(c_in[s], of_pair(c_in[s], pair))
                        for t in range(JT):
                            last = nc.tensor.transpose(misc[m % 2][0:CD, t * 128:(t + 1) * 128], ctx_sb[s][:, t, :], ident[:, :])
                        last.then_inc(misc_full, 1)
                    elif name == "lnT":
                        k, s = args
                        bank_free(m)
                        pe.wait_ge(xn_done, at(xn_done, ("norm", k, s)))
                        turn(m, xn[s], [128] * TT)
                    elif name == "xT":
                        s, = args
                        bank_free(m)
                        pe.wait_ge(x_by_row, at(x_by_row, ("ff2", s)))
                        turn(m, xn[s], [128] * TT)
                    elif name in ("q", "k"):
                        f, s = args
                        bank_free(m)
                        if f is TEXT:
                            pe.wait_ge(xh_done, at(xh_done, ("xT", s)))
                        else:
                            pe.wait_ge(*taken(("lnT", 0 if f is SELF else 1, s)))
                        project_T(m, (w_q if name == "q" else w_k)[f.name], hT[s], N)
                    elif name == "kctx":
                        f, s = args
                        pe.wait_ge(*taken(("ctxT", s)))
                        for o in range(2):
                            bank_free(m + o)
                            nc.tensor.matmul(misc[(m + o) % 2][0:HALF, :], w_k[f.name][:, o * HALF:(o + 1) * HALF], ctxT[s][:, :],
                                             start=True, stop=True).then_inc(misc_full, 1)
                    elif name == "v":
                        f, s = args
                        bank_free(m)
                        pe.wait_ge(*taken(("lnT", 0, s)))
                        project_tok(m, hT[s], w_v["self"])
                    elif name == "vctx":
                        f, s = args
                        for o in range(2):
                            bank_free(m + o)
                            for t in range(2):
                                last = nc.tensor.matmul(misc[(m + o) % 2][:, t * D:(t + 1) * D],
                                                        ctxT[s][:, (2 * o + t) * 128:(2 * o + t + 1) * 128], w_v[f.name][:, :],
                                                        start=True, stop=True)
                            last.then_inc(misc_full, 1)
                    elif name == "camq":
                        s, = args
                        bank_free(m)
                        pe.wait_ge(c_in[s], of_pair(c_in[s], pair))
                        for o in range(2):
                            last = nc.tensor.matmul(misc[m % 2][0:HALF, o * 256:o * 256 + NQA], w_qca[:, o * HALF:(o + 1) * HALF],
                                                    ca_sb[s][:, :], start=True, stop=True)
                        last.then_inc(misc_full, 1)
                    elif name == "cambc":
                        s, = args
                        pe.wait_ge(wide_done, at(wide_done, ("ctxT", s)))
                        for o in range(4):
                            bank_free(m + o)
                            for t in range(2):
                                last = nc.tensor.matmul(misc[(m + o) % 2][0:NQA, t * D:(t + 1) * D],
                                                        ca_wide[s][:, 2 * (o % 2) + t, :], thin["Wk_ca" if o < 2 else "Wv_ca"][:, :],
                                                        start=True, stop=True)
                            last.then_inc(misc_full, 1)
                    elif name == "outT":
                        f, s = args
                        bank_free(m)
                        pe.wait_ge(*taken(("EVT", last_group[f.name, s])))
                        turn(m, o_tok[s], [128] * TT)
                    elif name == "out":
                        f, s = args
                        bank_free(m)
                        pe.wait_ge(*taken(("outT", f.name, s)))
                        project_tok(m, oT[s], w_o[f.name])
                    elif name == "ff1":
                        s, j = args
                        bank_free(m)
                        pe.wait_ge(*taken(("lnT", 2, s)))
                        for o, col in enumerate((j * 128, FF + j * 128)):
                            for c in range(2):
                                last = nc.tensor.matmul(misc[m % 2][:, o * 256:(o + 1) * 256], w_ff1[:, c, col:col + 128],
                                                        hT[s][:, c, :], start=(c == 0), stop=(c == 1))
                        last.then_inc(misc_full, 1)
                    elif name == "ff2":
                        s, = args
                        bank_free(m)
                        pe.wait_ge(ff_done, at(ff_done, ("glu", s)))
                        for t in range(TT):
                            for j in range(FF // 128):
                                last = nc.tensor.matmul(misc[m % 2][:, t * D:(t + 1) * D], ff_a[:, j, t * 128:(t + 1) * 128],
                                                        w_ff2[:, j, :], start=(j == 0), stop=(j == FF // 128 - 1))
                        last.then_inc(misc_full, 1)
                    elif name == "cam2T":
                        s, = args
                        bank_free(m)
                        pe.wait_ge(*taken(("EVT", last_group["cam", s])))
                        turn(m, o_cam[s], [NQA])
                    elif name == "cam2q":
                        s, = args
                        bank_free(m)
                        pe.wait_ge(*taken(("cam2T", s)))
                        for c in range(2):
                            last = nc.tensor.matmul(misc[m % 2][0:NQA, 0:D], oT[s][:, c, 0:NQA], wide["Wq"][:, c, :],
                                                    start=(c == 0), stop=(c == 1))
                        last.then_inc(misc_full, 1)
                    elif name == "hsumT":
                        s, = args
                        bank_free(m)
                        pe.wait_ge(*taken(("EVT", last_group["text", s])))
                        pe.wait_ge(cam_done, at(cam_done, ("cam2", s, 5)))
                        for c in range(2):
                            for t in range(TT):
                                place = misc[m % 2][0:HALF, c * 256 + t * 128:c * 256 + (t + 1) * 128]
                                nc.tensor.matmul(place, cam_out[s][:, c * HALF:(c + 1) * HALF], pick[:, t * 128:(t + 1) * 128],
                                                 start=True, stop=False)
                                last = nc.tensor.matmul(place, o_tok[s][:, t, c * HALF:(c + 1) * HALF], ident[:, :],
                                                        start=False, stop=True)
                        last.then_inc(misc_full, 1)
                    elif name == "fin":
                        s, = args
                        bank_free(m)
                        pe.wait_ge(*taken(("hsumT", s)))
                        project_tok(m, oT[s], w_o["text"])
                    elif name == "MX":
                        n, fill = args
                        f, s, g = seq[n]
                        no = fill_no[args]
                        if g == 0 and fill == 0:
                            pe.wait_ge(rows_in[f.name][s], of_pair(rows_in[f.name][s], pair))
                        if no >= MX_BANKS:
                            pe.wait_ge(mx_read, of_pair(mx_read, pair, no - MX_BANKS))
                        elif seg is not BEFORE:
                            pe.wait_ge(mx_read, of_pair(mx_read, pair - 1, max(range(no, len(fill_no), MX_BANKS))))
                        for r in range(f.per_bank):
                            k, t = divmod(fill * f.per_bank + r, len(f.q_tiles))
                            q0, n_q = f.q_tiles[t]
                            last = nc.tensor.matmul(mx_bank[no % MX_BANKS][0:n_q, r * f.nk:(r + 1) * f.nk],
                                                    q_rows[f.name][s][0:f.max_rows, GH * g + k, q0:q0 + n_q],
                                                    k_rows[f.name][s][0:f.max_rows, GH * g + k, 0:f.nk], start=True, stop=True)
                        last.then_inc(mx_full, 1)
                    elif name == "MT":
                        n, = args
                        f, s, g = seq[n]
                        bank_free(m)
                        pe.wait_ge(m_split, of_pair(m_split, pair, n))
                        for t, (q0, n_q) in enumerate(f.q_tiles):
                            last = nc.tensor.transpose(misc[m % 2][:, :].bitcast(BF16)[0:2 * GH, q0:q0 + n_q],
                                                       m_parts[n % 2][0:n_q, t, :, :].rearrange("p a k -> p (a k)"), ident_bf[0:n_q, 0:n_q])
                        last.then_inc(misc_full, 1)
                    elif name == "ST":
                        n, p, u, k = args
                        f, s, g = seq[n]
                        no = GH * u + k
                        if p == 0 and k == 0:
                            pe.wait_ge(m_in[n % 2], of_pair(m_in[n % 2], pair, n))
                        if no >= ST_BANKS:
                            pe.wait_ge(exp_done, of_pair(exp_done, pair, no - ST_BANKS))
                        for half in range(2):
                            kt = 2 * p + half
                            ks = f.k_tiles[kt]
                            last = nc.tensor.matmul(st_bank[no % ST_BANKS][0:ks, half * f.nq:(half + 1) * f.nq],
                                                    k_rows[f.name][s][0:128, GH * g + k, kt * 128:kt * 128 + ks],
                                                    q_rows[f.name][s][0:128, GH * g + k, 0:f.nq], start=True, stop=True)
                        last.then_inc(st_full, 1)
                    elif name == "PV":
                        n, p, u = args
                        f, s, g = seq[n]
                        pe.wait_ge(exp_done, of_pair(exp_done, pair, GH * u + GH - 1))
                        if g == 0 and p == 0:
                            if f is CAM:
                                pe.wait_ge(cv_done, at(cv_done, ("xcopy", s)))
                            elif f is not SELF:
                                pe.wait_ge(*taken(("vctx", f.name, s), 1))
                        if p == 0 and n:
                            pe.wait_ge(o_read, of_pair(o_read, pair, n - 1))
                        for half in range(2):
                            kt = 2 * p + half
                            ks = f.k_tiles[kt]
                            for k in range(GH):
                                last = nc.tensor.matmul(o_bank[HW * k:HW * (k + 1), 0:f.nq], v_rows[f.name][s][0:ks, kt, GH * g + k, :],
                                                        probs[0:ks, u % P_RING, k, half * f.nq:(half + 1) * f.nq],
                                                        start=(kt == 0), stop=(kt == len(f.k_tiles) - 1))
                        last.then_inc(pv_done, 1)
                    elif name == "EVT":
                        n, = args
                        f, s, g = seq[n]
                        bank_free(m)
                        pe.wait_ge(o_read, of_pair(o_read, pair, n))
                        for t, (q0, n_q) in enumerate(f.q_tiles):
                            last = nc.tensor.transpose(misc[m % 2][0:n_q, t * 128:(t + 1) * 128], o_sb[n % 2][:, q0:q0 + n_q], ident[:, :])
                        last.then_inc(misc_full, 1)
                for e in "AD":
                    last_use = max(m for m, u_ in enumerate(seg.uses) if u_ == e)
                    pe.wait_ge(misc_taken[e], at(misc_taken[e], last_use))
                if seg is not BEFORE:
                    pe.wait_ge(exp_done, of_pair(exp_done, i, GH * n_units - 1))
                    pe.wait_ge(o_read, of_pair(o_read, i, n_groups - 1))

            run_round(BEFORE, -1)
            pe.wait_ge(w_in, 16 * N_WEIGHT_LOADS)
            pe.wait_ge(ready1, READY1)
            with pe.Fori(0, PAIRS - 1) as i:
                run_round(BODY, i)
            run_round(LAST, PAIRS - 1)

        @block.scalar
        def _(act):
            def lay_by_row(weights, done):
                for wt, f in weights:
                    chunks = wt.shape[1] if len(wt.shape) == 3 else 1
                    for c in range(chunks):
                        dst = wt[:, c, :] if len(wt.shape) == 3 else wt[:, :]
                        nc.scalar.copy(dst.rearrange("p (r h) -> p r h", h=f.heads),
                                       raw[wt.name][:, c * D:(c + 1) * D].rearrange("p (h r) -> p r h", h=f.heads)).then_inc(done, 1)

            act.wait_ge(w_first, 16 * N_FIRST_LOADS)
            lay_by_row(by_row[:2], ready0)
            act.wait_ge(ready0, READY0)
            def run_round(seg, i):
                def at(s, key):
                    return in_round(seg, i, s, key)

                def taken(step, o=0):
                    m = seg.use_no[step] + o
                    return misc_taken[seg.uses[m]], at(misc_taken[seg.uses[m]], m)

                for name, args, m, delta in seg.steps:
                    pair = i + delta
                    if name in ("ctxT", "lnT", "v", "outT", "cam2T", "cam2q", "hsumT", "MT") or name in SPLIT_STEPS and name != "kctx":
                        act.wait_ge(misc_full, at(misc_full, m))
                    if name == "ctxT":
                        s, = args
                        nc.scalar.copy(ctxT[s][:, :], misc[m % 2][0:CD, :]).then_inc(misc_taken["A"], 1)
                    elif name == "lnT":
                        k, s = args
                        for c in range(2):
                            last = nc.scalar.activation(hT[s][:, c, :], misc[m % 2][0:HALF, c * 256:(c + 1) * 256], ACT.Identity,
                                                        bias=shifts[:, k, c:c + 1], scale=gains[:, k, c:c + 1])
                        last.then_inc(misc_taken["A"], 1)
                    elif name in SPLIT_STEPS:
                        s = args[-1]
                        f = args[0] if name in ("q", "k", "kctx") else CAM
                        stored_before = {"q": {"cross": "self", "text": "cross", "self": "text"},
                                         "kctx": {"cross": "self", "text": "cross"}, "k": {"self": "text"}}.get(name, {}).get(f.name)
                        if stored_before and not (f is SELF and seg is BEFORE):
                            stored = parts_out[name[0], stored_before][s]
                            act.wait_ge(stored, of_pair(stored, i))
                            act.sem_inc(passed, 1)
                        if name == "xT":
                            nc.scalar.copy(hT[s][:, :, :], misc[m % 2][0:HALF, :].rearrange("p (c t) -> p c t", c=2)).then_inc(xh_done, 1)
                        for o in range(len(MISC_USES[name])):
                            if name == "kctx":
                                act.wait_ge(misc_full, at(misc_full, m + o))
                            dst, src = split_views(name, args, m, o)
                            nc.scalar.copy(dst[0], src).then_inc(hi_done, 1)
                    elif name in ("v", "vctx"):
                        f, s = args
                        for o in range(len(MISC_USES[name])):
                            if name == "vctx":
                                act.wait_ge(misc_full, at(misc_full, m + o))
                            elif seg is BEFORE and s == 1:
                                act.wait_ge(filled1, 2)
                                act.sem_inc(passed, 1)
                            nc.scalar.copy(v_rows[f.name][s][:, 2 * o:2 * o + 2, :, 0:f.dh],
                                           misc[(m + o) % 2][:, 0:2 * D].rearrange("p (t h d) -> p t h d", t=2, d=f.dh))\
                                .then_inc(misc_taken["A"], 1)
                    elif name in ("outT", "hsumT"):
                        s = args[-1]
                        nc.scalar.copy(oT[s][:, :, :], misc[m % 2][0:HALF, :].rearrange("p (c t) -> p c t", c=2))\
                            .then_inc(misc_taken["A"], 1)
                    elif name == "cam2T":
                        s, = args
                        nc.scalar.copy(oT[s][:, :, 0:NQA], misc[m % 2][0:HALF, :].rearrange("p (c t) -> p c t", c=2)[:, :, 0:NQA])\
                            .then_inc(misc_taken["A"], 1)
                    elif name == "cam2q":
                        nc.scalar.copy(cam_q[:, :].rearrange("p (h r) -> p r h", h=CAM.heads),
                                       misc[m % 2][0:NQA, 0:D].rearrange("p (r h) -> p r h", h=CAM.heads)).then_inc(misc_taken["A"], 1)
                    elif name == "cambc":
                        s, = args
                        for o in range(4):
                            act.wait_ge(misc_full, at(misc_full, m + o))
                            last = nc.scalar.copy((kb if o < 2 else vb)[:, 2 * (o % 2):2 * (o % 2) + 2, :],
                                                  misc[(m + o) % 2][0:NQA, 0:2 * D].rearrange("p (t d) -> p t d", t=2))
                            last.then_inc(misc_taken["A"], 1)
                    elif name == "ff1":
                        s, j = args
                        act.wait_ge(misc_full, at(misc_full, m))
                        nc.scalar.activation(ff_g[:, j, :], misc[m % 2][:, 256:512], ACT.Identity,
                                             bias=b_ff1[:, FF // 128 + j:FF // 128 + j + 1]).then_inc(gate_done, 1)
                        nc.scalar.activation(ff_a[:, j, :], misc[m % 2][:, 0:256], ACT.Identity, bias=b_ff1[:, j:j + 1])\
                            .then_inc(misc_taken["A"], 1)
                    elif name == "gelu":
                        s, = args
                        act.wait_ge(gate_done, at(gate_done, ("ff1", s, FF // 128 - 1)))
                        nc.scalar.activation(ff_g[:, :, :], ff_g[:, :, :], ACT.Gelu).then_inc(gelu_done, 1)
                    elif name == "cam2" and args[1] == 2:
                        s, _ = args
                        act.wait_ge(cam_arg, at(cam_arg, ("cam2", s, 1)))
                        nc.scalar.activation(cam_e[:, :, :], cam_d[:, :, :], ACT.Exp, scale=CAM.scale).then_inc(cam_exp, 1)
                    elif name == "MT":
                        n, = args
                        f, s, g = seq[n]
                        if n >= 2:
                            act.wait_ge(m_in[n % 2], of_pair(m_in[n % 2], pair, n - 2))
                        elif seg is not BEFORE:
                            act.wait_ge(m_in[n % 2], of_pair(m_in[n % 2], pair - 1, n_groups + n - 2))
                        nc.scalar.copy(mT[n % 2][:, 0:f.nq], misc[m % 2][:, :].bitcast(BF16)[0:2 * GH, 0:f.nq])\
                            .then_inc(misc_taken["A"], 1)
                    elif name == "EVC":
                        n, u = args
                        f, s, g = seq[n]
                        act.wait_ge(pv_done, of_pair(pv_done, pair, u))
                        nc.scalar.copy(o_sb[n % 2][:, 0:f.nq], o_bank[:, 0:f.nq]).then_inc(o_read, 1)
                    elif name == "MD":
                        n, = args
                        f, s, g = seq[n]
                        act.wait_ge(*taken(("MT", n)))
                        act.dma_start(q_rows[f.name][s][M_ROW:M_ROW + 2, GH * g:GH * g + GH, 0:f.nq],
                                      mT[n % 2][:, 0:f.nq]).then_inc(m_in[n % 2], 16)
                    elif name == "ST":
                        n, p, u, k = args
                        f, s, g = seq[n]
                        no = GH * u + k
                        act.wait_ge(st_full, of_pair(st_full, pair, no))
                        if k == 0 and u >= P_RING:
                            act.wait_ge(pv_done, of_pair(pv_done, pair, u - P_RING))
                        bank = st_bank[no % ST_BANKS]
                        short = f.k_tiles[2 * p + 1]
                        if short == 128:
                            last = nc.scalar.activation(probs[:, u % P_RING, k, 0:2 * f.nq], bank[:, 0:2 * f.nq], ACT.Exp, scale=f.scale)
                        else:
                            nc.scalar.activation(probs[:, u % P_RING, k, 0:f.nq], bank[:, 0:f.nq], ACT.Exp, scale=f.scale)
                            last = nc.scalar.activation(probs[0:short, u % P_RING, k, f.nq:2 * f.nq], bank[0:short, f.nq:2 * f.nq],
                                                        ACT.Exp, scale=f.scale)
                        last.then_inc(exp_done, 1)
                if seg is not BEFORE:
                    act.wait_ge(pv_done, of_pair(pv_done, i, n_units - 1))

            run_round(BEFORE, -1)
            act.wait_ge(w_in, 16 * N_WEIGHT_LOADS)
            lay_by_row(by_row[2:], ready1)
            act.wait_ge(ready1, READY1)
            with act.Fori(0, PAIRS - 1) as i:
                run_round(BODY, i)
            run_round(LAST, PAIRS - 1)

        @block.vector
        def _(dve):
            nc.vector.memset(v8[0][:, :, :, :], 1.0).then_inc(ready0, 1)
            dve.wait_ge(w_first, 16 * N_FIRST_LOADS)
            nc.vector.tensor_copy(ident_bf[:, :], ident[:, :]).then_inc(ready0, 1)
            def run_round(seg, i):
                def at(s, key):
                    return in_round(seg, i, s, key)

                def taken(step, o=0):
                    m = seg.use_no[step] + o
                    return misc_taken[seg.uses[m]], at(misc_taken[seg.uses[m]], m)

                links = 0

                def link(ins):
                    nonlocal links
                    links += 1
                    ins.then_inc(dve_step, 1)
                    dve.wait_ge(dve_step, at(dve_step, links - 1))
                    dve.sem_inc(passed, 1)

                for name, args, m, delta in seg.dve_steps:
                    pair = i + delta
                    if name == "ln":
                        k, s = args
                        if k == 0:
                            dve.wait_ge(x_in[s], of_pair(x_in[s], pair))
                        else:
                            dve.wait_ge(*taken(("out", ("self", "cross")[k - 1], s)))
                        nc.vector.bn_stats(stats[s][:, 0, :], x_sb[s][:, 0, :])
                        link(nc.vector.bn_stats(stats[s][:, 1, :], x_sb[s][:, 1, :]))
                        nc.vector.bn_aggr(mean_var[s][:, 0, :], stats[s][:, 0, :])
                        link(nc.vector.bn_aggr(mean_var[s][:, 1, :], stats[s][:, 1, :]))
                        nc.vector.tensor_scalar(var_eps[s][:, :], mean_var[s][:, :, 1], EPS, None, ALU.add).then_inc(var_done, 1)
                    elif name == "norm":
                        k, s = args
                        dve.wait_ge(rstd_done, at(rstd_done, ("ln", k, s)))
                        if k == 0 and seg is not BEFORE:
                            dve.wait_ge(misc_full, at(misc_full, seg.use_no["xT", s]))
                        for t in range(TT):
                            last = nc.vector.tensor_scalar(xn[s][:, t, :], x_sb[s][:, t, :], mean_var[s][:, t, 0:1], rstd[s][:, t:t + 1],
                                                           ALU.subtract, ALU.mult)
                        last.then_inc(xn_done, 1)
                        if seg is BEFORE and s == 1:
                            nc.vector.memset(k8[1][:, :, :].bitcast(F32), TWO_ONES).then_inc(filled1, 1)
                            nc.vector.memset(v8[1][:, :, :, :], 1.0).then_inc(filled1, 1)
                    elif name in SPLIT_STEPS:
                        for o in range(len(MISC_USES[name])):
                            no = seg.split_no[m] + o
                            dve.wait_ge(hi_done, at(hi_done, no))
                            if no >= 2:
                                dve.wait_ge(split_done, at(split_done, no - 2))
                            dst, src = split_views(name, args, m, o)
                            nc.vector.tensor_tensor(dst[1], src, dst[0], ALU.subtract).then_inc(mid_done, 1)
                            nc.vector.tensor_tensor(rest_view(no, dst[0]), src, dst[0], ALU.subtract)\
                                .then_inc(misc_taken["D"], 1)
                    elif name in ("out", "ff2"):
                        s = args[-1]
                        dve.wait_ge(misc_full, at(misc_full, m))
                        key = ("bias", 2 if name == "ff2" else 0 if args[0] is SELF else 1, s)
                        dve.wait_ge(xb_done, at(xb_done, key))
                        if name == "ff2":
                            dve.wait_ge(*taken(("lnT", 2, s)))
                            nc.vector.tensor_tensor(xn[s][:, :, :].rearrange("p t (r h) -> p t h r", h=CAM.heads),
                                                    misc[m % 2][:, 0:TT * D].rearrange("p (t h r) -> p t h r", t=TT, h=CAM.heads),
                                                    xb_sb[s][:, :, :].rearrange("p t (h r) -> p t h r", h=CAM.heads), ALU.add)\
                                .then_inc(x_by_row, 1)
                        nc.vector.tensor_tensor(x_sb[s][:, :, :], misc[m % 2][:, 0:TT * D].rearrange("p (t d) -> p t d", t=TT),
                                                xb_sb[s][:, :, :], ALU.add)\
                            .then_inc(misc_taken["D"], 1)
                    elif name == "glu":
                        s, = args
                        dve.wait_ge(gelu_done, at(gelu_done, ("gelu", s)))
                        dve.wait_ge(*taken(("ff1", s, FF // 128 - 1)))
                        nc.vector.tensor_tensor(ff_a[:, :, :], ff_a[:, :, :], ff_g[:, :, :], ALU.mult).then_inc(ff_done, 1)
                    elif name == "MX":
                        n, fill = args
                        f, s, g = seq[n]
                        no = fill_no[args]
                        if fill == 0 and n >= 2:
                            dve.wait_ge(m_split, of_pair(m_split, pair, n - 2))
                        elif fill == 0 and seg is not BEFORE:
                            dve.wait_ge(m_split, of_pair(m_split, pair - 1, n_groups + n - 2))
                        dve.wait_ge(mx_full, of_pair(mx_full, pair, no))
                        n_q = min(128, f.nq)
                        nc.vector.tensor_reduce(neg_max[n % 2][0:n_q, fill * f.per_bank:(fill + 1) * f.per_bank],
                                                mx_bank[no % MX_BANKS][0:n_q, 0:f.per_bank * f.nk].rearrange("p (r k) -> p r k", k=f.nk),
                                                X, ALU.max, negate=True).then_inc(mx_read, 1)
                    elif name == "NM":
                        n, = args
                        f, s, g = seq[n]
                        nqt = len(f.q_tiles)
                        n_q = min(128, f.nq)
                        view = neg_max[n % 2][0:n_q, 0:GH * nqt].rearrange("p (k t) -> p t k", t=nqt)
                        dve.wait_ge(mx_read, of_pair(mx_read, pair, fill_no[n, f.fills - 1]))
                        before_it = ("MT", (n - 2) % n_groups)
                        if before_it in seg.use_no and seg.use_no[before_it] < m:
                            dve.wait_ge(misc_full, at(misc_full, seg.use_no[before_it]))
                        link(nc.vector.tensor_copy(m_parts[n % 2][0:n_q, 0:nqt, 0, :], view))
                        nc.vector.tensor_tensor(m_parts[n % 2][0:n_q, 0:nqt, 1, :], view, m_parts[n % 2][0:n_q, 0:nqt, 0, :],
                                                ALU.subtract).then_inc(m_split, 1)
                    elif name == "EVT":
                        n, = args
                        f, s, g = seq[n]
                        nqt = len(f.q_tiles)
                        n_q = min(128, f.nq)
                        if n >= 2:
                            dve.wait_ge(*taken(("EVT", n - 2)))
                        dve.wait_ge(misc_full, at(misc_full, m))
                        view = misc[m % 2][0:n_q, 0:nqt * 128].rearrange("p (t k c) -> p t k c", t=nqt, k=GH)
                        link(nc.vector.reciprocal(recip[n % 2][0:n_q, 0:nqt, :], view[:, :, :, HW - 1]))
                        if f is CAM:
                            dst = o_cam[s][:, :, :].rearrange("p t (c h) -> p t h c", h=f.heads)[:, :, GH * g:GH * (g + 1), :]
                        else:
                            dst = o_tok[s][0:n_q, 0:nqt, GH * g * f.dh:GH * (g + 1) * f.dh].rearrange("p t (k c) -> p t k c", k=GH)
                        nc.vector.tensor_tensor(dst,
                                                view[:, :, :, 0:f.dh],
                                                recip[n % 2][0:n_q, 0:nqt, :].unsqueeze(3).broadcast_to([n_q, nqt, GH, f.dh]), ALU.mult)\
                            .then_inc(misc_taken["D"], 1)
                    elif name == "cam2":
                        s, phase = args
                        if phase == 1:
                            dve.wait_ge(cam_prod, at(cam_prod, ("cam2", s, 0)))
                            link(nc.vector.tensor_reduce(cam_s[:, :, :], cam_t[:, :, :].rearrange("p j (h d) -> p j h d", h=8), X, ALU.add))
                            link(nc.vector.tensor_reduce(cam_m[:, :], cam_s[:, :, :].rearrange("p j h -> p h j"), X, ALU.max))
                            nc.vector.tensor_tensor(cam_d[:, :, :], cam_s[:, :, :], cam_m[:, :].unsqueeze(1).broadcast_to([NQA, CA, 8]),
                                                    ALU.subtract).then_inc(cam_arg, 1)
                        elif phase == 3:
                            dve.wait_ge(cam_exp, at(cam_exp, ("cam2", s, 2)))
                            link(nc.vector.tensor_reduce(cam_z[:, :], cam_e[:, :, :].rearrange("p j h -> p h j"), X, ALU.add))
                            link(nc.vector.reciprocal(cam_z[:, :], cam_z[:, :]))
                            nc.vector.tensor_tensor(cam_e[:, :, :], cam_e[:, :, :], cam_z[:, :].unsqueeze(1).broadcast_to([NQA, CA, 8]),
                                                    ALU.mult).then_inc(cam_p, 1)
                        elif phase == 5:
                            dve.wait_ge(cam_pv, at(cam_pv, ("cam2", s, 4)))
                            nc.vector.tensor_reduce(cam_out[s][:, :], cam_t[:, :, :].rearrange("p j x -> p x j"), X, ALU.add).then_inc(cam_done, 1)
                    elif name == "fin":
                        s, = args
                        dve.wait_ge(misc_full, at(misc_full, m))
                        dve.wait_ge(xb_done, at(xb_done, ("xcopy", s)))
                        nc.vector.tensor_tensor(xb_sb[s][:, :, :], misc[m % 2][:, 0:TT * D].rearrange("p (t d) -> p t d", t=TT),
                                                xb_sb[s][:, :, :], ALU.add)\
                            .then_inc(misc_taken["D"], 1)
                assert links == seg.total[dve_step.name], links
                dve.wait_ge(split_done, at(split_done, seg.n_splits - 1))

            run_round(BEFORE, -1)
            with dve.Fori(0, PAIRS - 1) as i:
                run_round(BODY, i)
            run_round(LAST, PAIRS - 1)

        @block.gpsimd
        def _(pool):
            nc.gpsimd.memset(minus_half[:, :], -0.5).then_inc(ready0, 1)
            nc.gpsimd.memset(q8[0][:, :, :].bitcast(F32), 0.0).then_inc(ready0, 1)
            nc.gpsimd.memset(k8[0][:, :, :].bitcast(F32), TWO_ONES).then_inc(ready0, 1)
            nc.gpsimd.memset(q8[1][:, :, :].bitcast(F32), 0.0).then_inc(ready0, 1)
            pool.wait_ge(ready0, READY0)
            def run_round(seg, i):
                def at(s, key):
                    return in_round(seg, i, s, key)

                def taken(step, o=0):
                    m = seg.use_no[step] + o
                    return misc_taken[seg.uses[m]], at(misc_taken[seg.uses[m]], m)

                for name, args, m, delta in seg.steps:
                    pair = i + delta
                    if name == "ctxT":
                        s, = args
                        pool.wait_ge(*taken(("ctxT", s)))
                        pool.sem_inc(passed, 1)
                        nc.gpsimd.tensor_copy(ca_wide[s][:, :, :], ctxT[s][:, J - CA:J].unsqueeze(2).broadcast_to([CD, CA, NQA]))\
                            .then_inc(wide_done, 1)
                    elif name == "zeros":
                        s, = args
                        pool.wait_ge(*taken(("EVT", last_group["text", s])))
                        pool.sem_inc(passed, 1)
                        nc.gpsimd.memset(q8[s][:, 0:12, :].bitcast(F32), 0.0).then_inc(zeros_done, 1)
                    elif name == "ln":
                        k, s = args
                        pool.wait_ge(var_done, at(var_done, ("ln", k, s)))
                        nc.gpsimd.tensor_tensor(rstd[s][:, :], var_eps[s][:, :], minus_half[:, :], ALU.pow).then_inc(rstd_done, 1)
                    elif name == "bias":
                        k, s = args
                        if k == 0:
                            pool.wait_ge(y_out[s], 16 * i + 16)
                            pool.wait_ge(x_in[s], of_pair(x_in[s], pair))
                        bias = biases[("o1", "o2", "ff2")[k]]
                        nc.gpsimd.tensor_tensor(xb_sb[s][:, :, :], x_sb[s][:, :, :], bias[:, :].unsqueeze(1).broadcast_to([128, TT, D]),
                                                ALU.add).then_inc(xb_done, 1)
                    elif name == "xcopy":
                        s, = args
                        pool.wait_ge(*taken(("ff2", s)))
                        pool.sem_inc(passed, 1)
                        nc.gpsimd.tensor_copy(vc_[s][:, :, :, 0:CAM.dh], x_sb[s][:, :, :].rearrange("p t (h d) -> p t h d", d=CAM.dh))\
                            .then_inc(cv_done, 1)
                        nc.gpsimd.tensor_tensor(xb_sb[s][:, :, :], x_sb[s][:, :, :], biases["out"][:, :].unsqueeze(1).broadcast_to([128, TT, D]),
                                                ALU.add).then_inc(xb_done, 1)
                    elif name in SPLIT_STEPS:
                        for o in range(len(MISC_USES[name])):
                            no = seg.split_no[m] + o
                            pool.wait_ge(misc_taken["D"], at(misc_taken["D"], m + o))
                            dst, src = split_views(name, args, m, o)
                            rest_v = rest_view(no, dst[0])
                            pool.wait_ge(mid_done, at(mid_done, no))
                            nc.gpsimd.tensor_tensor(dst[2], rest_v, dst[1], ALU.subtract).then_inc(split_done, 1)
                    elif name == "cam2":
                        s, phase = args
                        if phase == 0:
                            pool.wait_ge(*taken(("cam2q", s)))
                            nc.gpsimd.tensor_tensor(cam_t[:, :, :], kb[:, :, :], cam_q[:, :].unsqueeze(1).broadcast_to([NQA, CA, D]), ALU.mult)\
                                .then_inc(cam_prod, 1)
                        elif phase == 4:
                            pool.wait_ge(cam_p, at(cam_p, ("cam2", s, 3)))
                            nc.gpsimd.tensor_tensor(cam_t[:, :, :].rearrange("p j (h d) -> p j h d", h=8),
                                                    vb[:, :, :].rearrange("p j (h d) -> p j h d", h=8),
                                                    cam_e[:, :, :].unsqueeze(3).broadcast_to([NQA, CA, 8, CAM.dh]), ALU.mult)\
                                .then_inc(cam_pv, 1)

            run_round(BEFORE, -1)
            pool.wait_ge(w_in, 16 * N_WEIGHT_LOADS)
            with pool.Fori(0, PAIRS - 1) as i:
                run_round(BODY, i)
            run_round(LAST, PAIRS - 1)


def kernel(**inputs):
    import numpy as _np
    import concourse.bacc as _bacc
    from concourse import mybir as _mybir
    from concourse.bass_utils import run_bass_kernel_spmd as _run

    nc = _bacc.Bacc("TRN2", target_bir_lowering=False, num_devices=1)
    arrays, aps = {}, {}

    def take(name, a):
        a = _np.ascontiguousarray(a)
        arrays[f"in_{name}_dram"] = a
        aps[name] = nc.dram_tensor(f"in_{name}_dram", a.shape, _mybir.dt.from_np(a.dtype), kind="ExternalInput").ap()

    take("x", inputs["x"])
    take("ctx", inputs["ctx_768"])
    for short, name in WEIGHTS.items():
        take(short, inputs[name])
    take("ident", _np.eye(128, dtype=_np.float32))
    rows = _np.linspace(0, NQA - 1, N).astype(_np.int64)
    take("pick", (_np.arange(NQA)[:, None] == rows[None, :]).astype(_np.float32))
    out = nc.dram_tensor("out_0_dram", (B, N, D), F32, kind="ExternalOutput").ap()
    two_blocks(nc, aps["x"], aps["ctx"], aps, out)
    r = _run(nc, [arrays], core_ids=[0])
    return r.results[0]["out_0_dram"]
```
